# Optimizing a Trainium2 kernel written in Bass

```python
import numpy as np
import jax
import jax.numpy as jnp

def _softmax(x, axis=-1):
    return jax.nn.softmax(x, axis=axis)

def _gelu(x):
    return jax.nn.gelu(x, approximate=True)

def _silu(x):
    return jax.nn.silu(x)

def _sigmoid(x):
    return jax.nn.sigmoid(x)

def _layernorm(x, axis=-1, eps=1e-05):
    m = jnp.mean(x, axis=axis, keepdims=True)
    v = jnp.var(x, axis=axis, keepdims=True)
    return (x - m) / jnp.sqrt(v + eps)

def _scatter_add(tgt, idx, src, axis=0):
    return tgt.at[idx].add(src)

def _segment_sum(src, seg, n):
    return jax.ops.segment_sum(src, seg, n)
kernel_name = 'mk_gnn_ffn_d2_gnn_r16_b27157'

def setup_inputs(seed: int=0):
    np.random.seed(seed)
    _w = jnp.asarray

    def _rec_inputs():
        import jax
        import jax.numpy as jnp
        _gk = jax.random.key(seed)
        x = -0.0003019 + 1 * jax.random.normal(jax.random.fold_in(_gk, 1), (1250, 1024), jnp.float32)
        src = jax.random.randint(jax.random.fold_in(_gk, 2), (20000,), 0, 1250, jnp.int32)
        dst = jax.random.randint(jax.random.fold_in(_gk, 3), (20000,), 0, 1250, jnp.int32)
        _o = jnp.argsort(dst, stable=True)
        src = src[_o]
        dst = dst[_o]
        return (x, src, dst)
    x, src, dst = _rec_inputs()

    def _L0_gnn_setup():
        import jax, jax.numpy as jnp
        import numpy as np
        N, IN_FEAT, OUT_FEAT, HEADS, E = (1250, 1024, 256, 4, 20000)
        NEG_SLOPE = 0.2
        key = jax.random.key(seed)
        k1, k2, k3, k4, k5, k6 = jax.random.split(key, 6)
        h = jax.random.normal(k1, (N, IN_FEAT), dtype=jnp.float32)
        src = jax.random.randint(k2, (E,), 0, N, dtype=jnp.int32)
        dst = jax.random.randint(k3, (E,), 0, N, dtype=jnp.int32)
        W = jax.random.normal(k4, (HEADS, IN_FEAT, OUT_FEAT), dtype=jnp.float32) * (1.0 / np.sqrt(IN_FEAT))
        a_l = jax.random.normal(k5, (HEADS, OUT_FEAT), dtype=jnp.float32) * (1.0 / np.sqrt(OUT_FEAT))
        a_r = jax.random.normal(k6, (HEADS, OUT_FEAT), dtype=jnp.float32) * (1.0 / np.sqrt(OUT_FEAT))
        return {'h': h, 'W': W, 'a_l': a_l, 'a_r': a_r, 'src': src, 'dst': dst}
    _L0_gnn_all = _L0_gnn_setup()
    _L0_gnn_in = {k: v for k, v in _L0_gnn_all.items() if k in ('W', 'a_l', 'a_r')}
    del _L0_gnn_all

    def _L0_ffn_setup():
        import jax, jax.numpy as jnp
        import numpy as np
        N_HEADS = 4
        RAILS = 64
        RAIL_W = 16
        MULT = 4
        N_EMBD = RAILS * RAIL_W
        B, T = (4, 128)
        key = jax.random.key(seed)
        k1, k2, k3, k4 = jax.random.split(key, 4)
        x = jax.random.normal(k1, (B, T, N_EMBD), dtype=jnp.float32)
        rail_maker = jax.random.normal(k2, (N_HEADS, RAILS, RAIL_W, RAIL_W), dtype=jnp.float32) * 0.02
        rail_up_proj = jax.random.normal(k3, (N_HEADS, RAILS, RAIL_W * MULT, RAIL_W), dtype=jnp.float32) * 0.02
        w_cproj = jax.random.normal(k4, (N_EMBD, N_EMBD * MULT * N_HEADS), dtype=jnp.float32) * 0.02
        return {'x': x, 'rail_maker': rail_maker, 'rail_up_proj': rail_up_proj, 'w_cproj': w_cproj}
    _L0_ffn_all = _L0_ffn_setup()
    _L0_ffn_in = {k: v for k, v in _L0_ffn_all.items() if k in ('rail_maker', 'rail_up_proj', 'w_cproj')}
    del _L0_ffn_all

    def _L1_gnn_setup():
        import jax, jax.numpy as jnp
        import numpy as np
        N = 1250
        E = 20000
        D_IN = 1024
        D_OUT = 1024
        key = jax.random.key(seed)
        k1, k2, k3, k4 = jax.random.split(key, 4)
        x = jax.random.normal(k1, (N, D_IN), dtype=jnp.float32)
        edge_index = jax.random.randint(k2, (2, E), 0, N, dtype=jnp.int64)
        W = jax.random.normal(k3, (D_OUT, D_IN), dtype=jnp.float32) * (1.0 / np.sqrt(D_IN))
        b = jax.random.normal(k4, (D_OUT,), dtype=jnp.float32) * 0.01
        return {'x': x, 'edge_index': edge_index, 'W': W, 'b': b}
    _L1_gnn_all = _L1_gnn_setup()
    _L1_gnn_in = {k: v for k, v in _L1_gnn_all.items() if k in ('W', 'b')}
    del _L1_gnn_all

    def _L1_ffn_setup():
        import jax, jax.numpy as jnp
        import numpy as np
        HIDDEN = 1024
        INTER = 256
        N_EXPERTS = 8

        def geglu(x, w1, w2, w3):
            return jax.nn.gelu(x @ w1, approximate=False) * (x @ w2) @ w3
        key = jax.random.key(seed)
        ks = jax.random.split(key, 8)
        s = 0.02
        x = jax.random.normal(ks[0], (2, 128, HIDDEN), dtype=jnp.float32)
        w1s = jax.random.normal(ks[1], (HIDDEN, INTER), dtype=jnp.float32) * s
        w2s = jax.random.normal(ks[2], (HIDDEN, INTER), dtype=jnp.float32) * s
        w3s = jax.random.normal(ks[3], (INTER, HIDDEN), dtype=jnp.float32) * s
        W1 = jax.random.normal(ks[4], (N_EXPERTS, HIDDEN, INTER), dtype=jnp.float32) * s
        W2 = jax.random.normal(ks[5], (N_EXPERTS, HIDDEN, INTER), dtype=jnp.float32) * s
        W3 = jax.random.normal(ks[6], (N_EXPERTS, INTER, HIDDEN), dtype=jnp.float32) * s
        Wg = jax.random.normal(ks[7], (HIDDEN, N_EXPERTS), dtype=jnp.float32) * s
        return {'x': x, 'w1s': w1s, 'w2s': w2s, 'w3s': w3s, 'W1': W1, 'W2': W2, 'W3': W3, 'Wg': Wg}
    _L1_ffn_all = _L1_ffn_setup()
    _L1_ffn_in = {k: v for k, v in _L1_ffn_all.items() if k in ('w1s', 'w2s', 'w3s', 'W1', 'W2', 'W3', 'Wg')}
    del _L1_ffn_all
    return {'x': x, 'src': src, 'dst': dst, 'L0_gnn_W': _L0_gnn_in['W'], 'L0_gnn_a_l': _L0_gnn_in['a_l'], 'L0_gnn_a_r': _L0_gnn_in['a_r'], 'L0_ffn_rail_maker': _L0_ffn_in['rail_maker'], 'L0_ffn_rail_up_proj': _L0_ffn_in['rail_up_proj'], 'L0_ffn_w_cproj': _L0_ffn_in['w_cproj'], 'L1_gnn_W': _L1_gnn_in['W'], 'L1_gnn_b': _L1_gnn_in['b'], 'L1_ffn_w1s': _L1_ffn_in['w1s'], 'L1_ffn_w2s': _L1_ffn_in['w2s'], 'L1_ffn_w3s': _L1_ffn_in['w3s'], 'L1_ffn_W1': _L1_ffn_in['W1'], 'L1_ffn_W2': _L1_ffn_in['W2'], 'L1_ffn_W3': _L1_ffn_in['W3'], 'L1_ffn_Wg': _L1_ffn_in['Wg']}

def reference(x, src, dst, L0_gnn_W, L0_gnn_a_l, L0_gnn_a_r, L0_ffn_rail_maker, L0_ffn_rail_up_proj, L0_ffn_w_cproj, L1_gnn_W, L1_gnn_b, L1_ffn_w1s, L1_ffn_w2s, L1_ffn_w3s, L1_ffn_W1, L1_ffn_W2, L1_ffn_W3, L1_ffn_Wg):
    import jax
    import jax.numpy as jnp

    def _L0_gnn_ref(h, W, a_l, a_r, src, dst):
        import jax, jax.numpy as jnp
        import numpy as np
        N, IN_FEAT, OUT_FEAT, HEADS, E = (1250, 1024, 256, 4, 20000)
        NEG_SLOPE = 0.2
        z = jnp.einsum('ni,hif->nhf', h, W)
        el = jnp.einsum('nhf,hf->nh', z, a_l)
        er = jnp.einsum('nhf,hf->nh', z, a_r)
        e = jax.nn.leaky_relu(el[src] + er[dst], NEG_SLOPE)
        m = jax.ops.segment_max(e, dst, num_segments=N)
        ex = jnp.exp(e - m[dst])
        s = jax.ops.segment_sum(ex, dst, num_segments=N)
        alpha = ex / s[dst]
        out = jax.ops.segment_sum(alpha[:, :, None] * z[src], dst, num_segments=N)
        return out.reshape(N, HEADS * OUT_FEAT)

    def _L0_ffn_ref(x, rail_maker, rail_up_proj, w_cproj):
        import jax, jax.numpy as jnp
        import numpy as np
        N_HEADS = 4
        RAILS = 64
        RAIL_W = 16
        MULT = 4
        N_EMBD = RAILS * RAIL_W
        B, T = (4, 128)
        b, t, _ = x.shape
        xr = x.reshape(b, t, RAILS, RAIL_W)
        y = jnp.einsum('btri,hrij->bthrj', xr, rail_maker)
        z = jnp.einsum('bthrj,hrkj->bthrk', y, rail_up_proj)
        h = jax.nn.gelu(z.reshape(b, t, -1), approximate=False)
        out = h @ w_cproj.T
        return out

    def _L1_gnn_ref(x, edge_index, W, b):
        import jax, jax.numpy as jnp
        import numpy as np
        N = 1250
        E = 20000
        D_IN = 1024
        D_OUT = 1024
        num_nodes = x.shape[0]
        self_idx = jnp.arange(num_nodes, dtype=edge_index.dtype)
        ei = jnp.concatenate([edge_index, jnp.stack([self_idx, self_idx], axis=0)], axis=1)
        row, col = (ei[0], ei[1])
        h = jnp.einsum('nd,od->no', x, W) + b
        deg = jnp.zeros((num_nodes,), dtype=h.dtype).at[row].add(1.0)
        deg_inv_sqrt = deg ** (-0.5)
        norm = deg_inv_sqrt[row] * deg_inv_sqrt[col]
        msg = norm[:, None] * h[col]
        out = jax.ops.segment_sum(msg, row, num_segments=num_nodes)
        return out

    def _L1_ffn_ref(x, w1s, w2s, w3s, W1, W2, W3, Wg):
        import jax, jax.numpy as jnp
        import numpy as np
        HIDDEN = 1024
        INTER = 256
        N_EXPERTS = 8

        def geglu(x, w1, w2, w3):
            return jax.nn.gelu(x @ w1, approximate=False) * (x @ w2) @ w3
        B, T, C = x.shape
        xf = x.reshape(-1, C)
        shared = geglu(xf, w1s, w2s, w3s)
        logits = xf @ Wg
        idx = jnp.argmax(logits, axis=-1)
        final = jnp.zeros_like(xf)
        for e in range(N_EXPERTS):
            y = geglu(xf, W1[e], W2[e], W3[e])
            final = final + jnp.where((idx == e)[:, None], y, 0.0)
        return (shared + final).reshape(B, T, C)
    edge_index = jnp.stack([src, dst])
    x = x + _L0_gnn_ref(_layernorm(x, axis=-1), L0_gnn_W, L0_gnn_a_l, L0_gnn_a_r, src, dst)
    x = x + _L0_ffn_ref(_layernorm(x, axis=-1)[None], L0_ffn_rail_maker, L0_ffn_rail_up_proj, L0_ffn_w_cproj)[0]
    x = x + _L1_gnn_ref(_layernorm(x, axis=-1), edge_index, L1_gnn_W, L1_gnn_b)
    x = x + _L1_ffn_ref(_layernorm(x, axis=-1)[None], L1_ffn_w1s, L1_ffn_w2s, L1_ffn_w3s, L1_ffn_W1, L1_ffn_W2, L1_ffn_W3, L1_ffn_Wg)[0]
    return x

_drawn_inputs = setup_inputs


def setup_inputs(seed=0):
    import zlib

    import numpy as np

    out = dict(_drawn_inputs(seed))
    spreads = {}
    factors = {'L0_ffn_rail_maker': 5.476,
     'L0_ffn_rail_up_proj': 5.202,
     'L0_ffn_w_cproj': 5.906,
     'L1_gnn_b': 4.796}
    for name, (base, spread) in spreads.items():
        noise = np.random.default_rng([zlib.crc32(name.encode()), seed]).standard_normal(out[name].shape)
        drawn = base * np.exp(spread * noise) if base else spread * noise
        out[name] = jnp.asarray(drawn.astype(out[name].dtype))
    for name, factor in factors.items():
        out[name] = (out[name] * factor).astype(out[name].dtype)
    return out
```

```python
from contextlib import ExitStack

import concourse.bass as bass
from concourse import mybir

F32 = mybir.dt.float32
F32R = mybir.dt.float32r
F16 = mybir.dt.float16
I32 = mybir.dt.int32
U16 = mybir.dt.uint16
ALU = mybir.AluOpType
ACT = mybir.ActivationFunctionType
AX = mybir.AxisListType

NODES = 1250
DIM = 1024
EDGES = 20000
HEADS = 4
P = 125
TILES = NODES // P
CHUNKS = EDGES // P
GROUP = 4
GROUPS = CHUNKS // GROUP
HEAD_F = DIM // HEADS
KT = DIM // 128
BANK = 512
RAILS = 64
RAIL_W = 16
RAIL_UP = 64
PAIRS = RAILS // 2
EXPERTS = 8
INTER = 256
SLOT = 128
SLOTS = (NODES - EXPERTS) // SLOT + EXPERTS
SLOPE = 0.2
EPS = 1e-5
FAR = -1e30


class Core:

    spent = []

    def __init__(self, nc, ctx, stage):
        self.nc, self.ctx, self.stage = nc, ctx, stage

    def sb(self, name, shape, dt):
        return self.ctx.enter_context(self.nc.sbuf_tensor(f"{self.stage}_{name}", shape, dt))

    def ps(self, name, shape):
        return self.ctx.enter_context(self.nc.psum_tensor(f"{self.stage}_{name}", shape, F32))

    def sem(self, name):
        semaphore = self.nc.alloc_semaphore(f"{self.stage}_{name}")
        self.spent.append(semaphore)
        return semaphore


def recycle(nc):
    nc.clear_and_free_semaphores(list(Core.spent))
    Core.spent.clear()
    nc.all_engine_barrier()


def constants(nc, keep, x, X, ident):
    x_in, ident_zero, ident_set = keep.sem("x_in"), keep.sem("ident_zero"), keep.sem("ident_set")
    with nc.Block() as block:

        @block.sync
        def _(sp):
            sp.dma_start(X[:], x.rearrange("(t p) d -> p t d", p=P)).then_inc(x_in, 16)
            sp.wait_ge(x_in, 16)

        @block.gpsimd
        def _(pool):
            nc.gpsimd.memset(ident[:], 0.0).then_inc(ident_zero, 1)
            pool.wait_ge(ident_zero, 1)
            nc.gpsimd.affine_select(out=ident[:], in_=ident[:], compare_op=ALU.not_equal, fill=1.0, base=0,
                                    pattern=[[-1, 128]], channel_multiplier=1).then_inc(ident_set, 1)
            pool.wait_ge(ident_set, 1)


def count_edges(nc, src, dst, ident, counts, counts_t):
    with ExitStack() as ctx:
        c = Core(nc, ctx, "count")
        src_i, dst_i = c.sb("src_i", [P, CHUNKS], I32), c.sb("dst_i", [P, CHUNKS], I32)
        src_f, dst_f = c.sb("src_f", [P, 2 * CHUNKS], F32), c.sb("dst_f", [P, 2 * CHUNKS], F32)
        iota_i = c.sb("iota_i", [P, NODES], I32)
        iota_h = c.sb("iota_h", [P, NODES], F16)
        zeros_h = c.sb("zeros_h", [P, P], F16)
        hot_src = [c.sb(f"hot_src{k}", [P, NODES], F16) for k in range(GROUP)]
        hot_dst = [c.sb(f"hot_dst{k}", [P, P], F16) for k in range(GROUP)]
        count_f = c.sb("count_f", [P, NODES], F32)
        count_u = c.sb("count_u", [P, NODES], U16)
        count_tu = c.sb("count_tu", [P, TILES, P], U16)
        ends = c.sb("ends", [P, 2 * GROUPS], F32)
        ends_all = c.sb("ends_all", [P, 2 * GROUPS], F32)
        tile_start_i, tile_start = c.sb("tile_start_i", [1, TILES, GROUPS], I32), c.sb("tile_start", [1, TILES, GROUPS], F32)
        group_up_i, group_up = c.sb("group_up_i", [1, TILES, GROUPS], I32), c.sb("group_up", [1, TILES, GROUPS], F32)
        group_down_i, group_down = c.sb("group_down_i", [1, TILES, GROUPS], I32), c.sb("group_down", [1, TILES, GROUPS], F32)
        before_i, before = c.sb("before_i", [1, TILES, TILES], I32), c.sb("before", [1, TILES, TILES], F32)
        reach_hi = c.sb("reach_hi", [1, TILES, GROUPS], F32)
        reach_lo = c.sb("reach_lo", [1, TILES, GROUPS], F32)
        meets = c.sb("meets", [1, TILES, GROUPS], F32)
        up_val, down_val = c.sb("up_val", [1, TILES, GROUPS], F32), c.sb("down_val", [1, TILES, GROUPS], F32)
        low, low1, high = c.sb("low", [1, TILES], F32), c.sb("low1", [1, TILES], F32), c.sb("high", [1, TILES], F32)
        last, width = c.sb("last", [1, TILES], F32), c.sb("width", [1, TILES], F32)
        earlier = c.sb("earlier", [1, TILES, TILES], F32)
        offset = c.sb("offset", [1, TILES], F32)
        bounds = c.sb("bounds", [1, 3, TILES], I32)
        ps_count = c.ps("ps_count", [P, 3 * BANK])
        ps_t = c.ps("ps_t", [P, 3, BANK])
        edges_in, iotas, floats = c.sem("edges_in"), c.sem("iotas"), c.sem("floats")
        ends_mine, ends_out = c.sem("ends_mine"), c.sem("ends_out")
        step, bounds_out = c.sem("bound_step"), c.sem("bounds_out")
        hot_ready, hot_used = c.sem("hot_ready"), c.sem("hot_used")
        counted, f_ready, u_ready = c.sem("counted"), c.sem("f_ready"), c.sem("u_ready")
        turned, tu_ready = c.sem("turned"), c.sem("tu_ready")
        u_stored, tu_stored = c.sem("u_stored"), c.sem("tu_stored")
        sync_tick, pool_tick = c.sem("sync_tick"), c.sem("pool_tick")
        columns = [(0, BANK), (BANK, 2 * BANK), (2 * BANK, NODES)]

        def load_bounds(eng, t):
            first = eng.value_load(bounds[0:1, 0, bass.ds(t, 1)], min_val=0, max_val=GROUPS - 1)
            groups = eng.value_load(bounds[0:1, 1, bass.ds(t, 1)], min_val=1, max_val=GROUPS)
            done = eng.value_load(bounds[0:1, 2, bass.ds(t, 1)], min_val=0, max_val=CHUNKS * TILES)
            return first, groups, done

        with nc.Block() as block:

            @block.sync
            def _(sp):
                sp.dma_start(src_i[:], src).then_inc(edges_in, 16)
                sp.dma_start(dst_i[:], dst).then_inc(edges_in, 16)
                sp.sem_inc(u_stored, 16)
                sp.sem_inc(tu_stored, 16)
                with sp.Fori(0, TILES) as t:
                    sp.wait_ge(u_ready, t + 1)
                    sp.sem_inc(sync_tick, 1)
                    sp.dma_start(counts[bass.ds(t * P, P), :], count_u[:]).then_inc(u_stored, 16)
                    sp.wait_ge(tu_ready, t + 1)
                    sp.sem_inc(sync_tick, 1)
                    sp.dma_start(counts_t.rearrange("(j p) d -> p j d", p=P)[:, :, bass.ds(t * P, P)],
                                 count_tu[:]).then_inc(tu_stored, 16)
                sp.wait_ge(u_stored, 16 * (TILES + 1))
                sp.wait_ge(tu_stored, 16 * (TILES + 1))

            @block.gpsimd
            def _(pool):
                nc.gpsimd.iota(iota_i[:], [[1, NODES]], base=0, channel_multiplier=0).then_inc(iotas, 1)
                nc.gpsimd.iota(tile_start_i[:], [[P, TILES], [0, GROUPS]], base=0, channel_multiplier=0).then_inc(iotas, 1)
                nc.gpsimd.iota(group_up_i[:], [[0, TILES], [1, GROUPS]], base=1, channel_multiplier=0).then_inc(iotas, 1)
                nc.gpsimd.iota(group_down_i[:], [[0, TILES], [-1, GROUPS]], base=GROUPS - 1, channel_multiplier=0).then_inc(iotas, 1)
                nc.gpsimd.iota(before_i[:], [[-1, TILES], [1, TILES]], base=0, channel_multiplier=0).then_inc(iotas, 1)
                nc.gpsimd.memset(zeros_h[:], 0.0).then_inc(iotas, 1)
                pool.wait_ge(ends_mine, 2)
                nc.gpsimd.partition_all_reduce(ends_all[:], ends[:], P, bass.bass_isa.ReduceOp.max).then_inc(ends_out, 1)
                with pool.Fori(0, TILES) as t:
                    pool.wait_ge(f_ready, t + 1)
                    pool.wait_ge(u_stored, 16 * t + 16)
                    pool.sem_inc(pool_tick, 1)
                    nc.gpsimd.tensor_copy(count_u[:], count_f[:]).then_inc(u_ready, 1)

            @block.vector
            def _(dve):
                dve.wait_ge(edges_in, 32)
                nc.vector.tensor_copy(src_f[:, 0:CHUNKS], src_i[:]).then_inc(floats, 1)
                nc.vector.tensor_copy(dst_f[:, 0:CHUNKS], dst_i[:]).then_inc(floats, 1)
                dve.wait_ge(floats, 2)
                by_group = dst_f[:, 0:CHUNKS].rearrange("p (g c) -> p g c", c=GROUP)
                nc.vector.tensor_reduce(ends[:, 0:GROUPS], by_group, AX.X, ALU.max).then_inc(ends_mine, 1)
                nc.vector.tensor_reduce(ends[:, GROUPS:2 * GROUPS], by_group, AX.X, ALU.min).then_inc(floats, 1)
                dve.wait_ge(floats, 3)
                nc.vector.tensor_scalar(ends[:, GROUPS:2 * GROUPS], ends[:, GROUPS:2 * GROUPS], -1.0, None,
                                        ALU.mult).then_inc(ends_mine, 1)
                dve.wait_ge(iotas, 6)
                nc.vector.tensor_copy(iota_h[:], iota_i[:])
                nc.vector.tensor_copy(tile_start[:], tile_start_i[:])
                nc.vector.tensor_copy(group_up[:], group_up_i[:])
                nc.vector.tensor_copy(group_down[:], group_down_i[:])
                nc.vector.tensor_copy(before[:], before_i[:]).then_inc(step, 1)
                dve.wait_ge(step, 1)
                dve.wait_ge(ends_out, 1)
                most = ends_all[0:1, 0:GROUPS].unsqueeze(1).broadcast_to((1, TILES, GROUPS))
                least = ends_all[0:1, GROUPS:2 * GROUPS].unsqueeze(1).broadcast_to((1, TILES, GROUPS))
                nc.vector.tensor_tensor(reach_hi[:], most, tile_start[:], ALU.is_ge)
                nc.vector.tensor_tensor(reach_lo[:], least, tile_start[:], ALU.add).then_inc(step, 1)
                dve.wait_ge(step, 2)
                nc.vector.scalar_tensor_tensor(meets[:], reach_lo[:], float(1 - P), reach_hi[:], ALU.is_ge,
                                               ALU.mult).then_inc(step, 1)
                dve.wait_ge(step, 3)
                nc.vector.tensor_tensor(up_val[:], meets[:], group_up[:], ALU.mult)
                nc.vector.tensor_tensor(down_val[:], meets[:], group_down[:], ALU.mult).then_inc(step, 1)
                dve.wait_ge(step, 4)
                nc.vector.tensor_reduce(high[:], up_val[:], AX.X, ALU.max)
                nc.vector.tensor_reduce(low1[:], down_val[:], AX.X, ALU.max).then_inc(step, 1)
                dve.wait_ge(step, 5)
                nc.vector.tensor_scalar(low[:], low1[:], -1.0, float(GROUPS - 1), ALU.mult, ALU.add).then_inc(step, 1)
                dve.wait_ge(step, 6)
                nc.vector.scalar_tensor_tensor(last[:], low[:], 1.0, high[:], ALU.add, ALU.max).then_inc(step, 1)
                dve.wait_ge(step, 7)
                nc.vector.tensor_tensor(width[:], last[:], low[:], ALU.subtract).then_inc(step, 1)
                dve.wait_ge(step, 8)
                nc.vector.scalar_tensor_tensor(earlier[:], before[:], 0.0,
                                               width[:].unsqueeze(1).broadcast_to((1, TILES, TILES)),
                                               ALU.is_lt, ALU.mult).then_inc(step, 1)
                dve.wait_ge(step, 9)
                nc.vector.tensor_reduce(offset[:], earlier[:], AX.X, ALU.add).then_inc(step, 1)
                dve.wait_ge(step, 10)
                nc.vector.tensor_copy(bounds[:, 0, :], low[:])
                nc.vector.tensor_copy(bounds[:, 1, :], width[:])
                nc.vector.tensor_scalar(bounds[:, 2, :], offset[:], float(GROUP), None, ALU.mult).then_inc(bounds_out, 1)
                dve.wait_ge(bounds_out, 1)
                with dve.Fori(0, TILES) as t:
                    first, groups, done = load_bounds(dve, t)
                    with dve.Fori(0, groups) as g:
                        for k in range(GROUP):
                            dve.wait_ge(hot_used, done + g * GROUP + (k + 1))
                            nc.vector.tensor_scalar(hot_src[k][:], iota_h[:], src_f[:, bass.ds((first + g) * GROUP + k, 1)], None,
                                                    ALU.is_equal)
                            nc.vector.tensor_scalar(hot_dst[k][:], iota_h[:, bass.ds(t * P, P)],
                                                    dst_f[:, bass.ds((first + g) * GROUP + k, 1)], None,
                                                    ALU.is_equal).then_inc(hot_ready, 1)

            @block.tensor
            def _(pe):
                pe.sem_inc(hot_used, GROUP)
                pe.wait_ge(bounds_out, 1)
                with pe.Fori(0, TILES) as t:
                    first, groups, done = load_bounds(pe, t)
                    for a, b in columns:
                        nc.tensor.matmul(ps_count[:, a:b], zeros_h[:], iota_h[:, a:b], start=True, stop=False)
                    with pe.Fori(0, groups) as g:
                        for k in range(GROUP):
                            pe.wait_ge(hot_ready, done + g * GROUP + (k + 1))
                            for a, b in columns:
                                mm = nc.tensor.matmul(ps_count[:, a:b], hot_dst[k][:], hot_src[k][:, a:b],
                                                      start=False, stop=False)
                            mm.then_inc(hot_used, 1)
                    for a, b in columns:
                        mm = nc.tensor.matmul(ps_count[:, a:b], zeros_h[:], iota_h[:, a:b], start=False, stop=True)
                    mm.then_inc(counted, 1)
                    pe.wait_ge(f_ready, t + 1)
                    for j in range(TILES):
                        mm = nc.tensor.transpose(ps_t[:, j // 4, (j % 4) * P:(j % 4 + 1) * P],
                                                 count_f[:, j * P:(j + 1) * P], ident[0:P, 0:P])
                    mm.then_inc(turned, 1)

            @block.scalar
            def _(act):
                with act.Fori(0, TILES) as t:
                    act.wait_ge(counted, t + 1)
                    act.wait_ge(tu_stored, 16 * t + 16)
                    act.wait_ge(u_stored, 16 * t + 16)
                    nc.scalar.copy(count_f[:], ps_count[:, 0:NODES]).then_inc(f_ready, 1)
                    act.wait_ge(turned, t + 1)
                    for a, b in ((0, 4), (4, 8), (8, TILES)):
                        cp = nc.scalar.copy(count_tu[:, a:b, :].rearrange("p a b -> p (a b)"),
                                            ps_t[:, a // 4, 0:(b - a) * P])
                    cp.then_inc(tu_ready, 1)


def layer_stats(nc, stage, X, mean_var, rstd):
    with ExitStack() as ctx:
        c = Core(nc, ctx, stage)
        parts = c.sb("stat_parts", [P, TILES, 2, 6], F32)
        std = c.sb("stat_std", [P, TILES], F32)
        eps = c.sb("stat_eps", [P, 1], F32)
        parts_in, stats_in, std_in, done = c.sem("parts_in"), c.sem("stats_in"), c.sem("std_in"), c.sem("rstd_in")
        with nc.Block() as block:

            @block.vector
            def _(dve):
                nc.vector.memset(eps[:], EPS)
                for t in range(TILES):
                    for half in range(2):
                        st = nc.vector.bn_stats(parts[:, t, half, :], X[:, t, half * BANK:(half + 1) * BANK])
                st.then_inc(parts_in, 1)
                dve.wait_ge(parts_in, 1)
                for t in range(TILES):
                    st = nc.vector.bn_aggr(mean_var[:, t, :], parts[:, t, :, :])
                st.then_inc(stats_in, 1)
                dve.wait_ge(std_in, 1)
                nc.vector.reciprocal(rstd[:], std[:]).then_inc(done, 1)
                dve.wait_ge(done, 1)

            @block.scalar
            def _(act):
                act.wait_ge(stats_in, 1)
                nc.scalar.activation(std[:], mean_var[:, :, 1], ACT.Sqrt, bias=eps[:]).then_inc(std_in, 1)


def by_twos(eng, step):
    with eng.Fori(0, TILES // 2 - 1) as i:
        step(i, 0, False)
        step(i, 1, False)
    step(TILES // 2 - 1, 0, False)
    step(TILES // 2 - 1, 1, True)


SPLIT = (("hi", "hi"), ("hi", "lo"), ("lo", "hi"))


def node_linear(nc, kind, X, mean_var, rstd, ident, w, out_hi, out_lo, extra):
    with ExitStack() as ctx:
        c = Core(nc, ctx, kind)
        w_land = [c.sb(f"w_land{k}", [128, DIM], F32) for k in range(2)]
        w_part = {n: c.sb(f"w_{n}", [128, KT, DIM], F32R) for n in ("hi", "lo")}
        xn = [c.sb(f"xn{k}", [P, DIM], F32) for k in range(2)]
        xt = [{n: c.sb(f"xt_{n}{k}", [128, KT, P], F32R) for n in ("hi", "lo")} for k in range(2)]
        z = [{n: c.sb(f"z_{n}{k}", [P, DIM], F32R) for n in ("hi", "lo")} for k in range(2)]
        rows = c.sb("rows", [P, 2, DIM], F32)
        mixed = c.sb("mixed", [P, 2, DIM], F32)
        ps_x = [c.ps(f"ps_x{h}", [128, 4, 128]) for h in range(2)]
        ps_z = [c.ps(f"ps_z{k}", [P, 2 * BANK]) for k in range(2)]
        w_in = [c.sem(f"w_in{k}") for k in range(2)]
        rows_in, w_hi_set, w_lo_set = c.sem("rows_in"), c.sem("w_hi_set"), c.sem("w_lo_set")
        xn_set, turned, xt_hi_set, xt_lo_set = c.sem("xn_set"), c.sem("xt_turned"), c.sem("xt_hi_set"), c.sem("xt_lo_set")
        z_sum, z_hi_set, z_lo_set = c.sem("z_sum"), c.sem("z_hi_set"), c.sem("z_lo_set")
        z_stored = [c.sem(f"z_stored{k}") for k in range(2)]
        mixed_set, dots_set, sync_tick = c.sem("mixed_set"), c.sem("dots_set"), c.sem("sync_tick")
        dots_out, act_tick = c.sem("dots_out"), c.sem("act_tick")
        dots = c.sb("dots", [P, 2, HEADS], F32)
        row_list = extra[:2] if kind == "attention" else extra[:1]

        with nc.Block() as block:

            @block.sync
            def _(sp):
                for k in range(KT):
                    if k >= 2:
                        sp.wait_ge(w_lo_set, k - 1)
                    sp.dma_start(w_land[k % 2][:], w[k * 128:(k + 1) * 128, :]).then_inc(w_in[k % 2], 16)
                for n, row in enumerate(row_list):
                    sp.dma_start(rows[:, n, :], row.partition_broadcast(P)).then_inc(rows_in, 16)
                for b in range(2):
                    sp.sem_inc(z_stored[b], 32)

                def step(i, b, last):
                    t = 2 * i + b
                    sp.wait_ge(z_hi_set, 2 * t + 2)
                    sp.sem_inc(sync_tick, 1)
                    sp.dma_start(out_hi[bass.ds(t * P, P), :], z[b]["hi"][:].bitcast(F32)).then_inc(z_stored[b], 16)
                    sp.wait_ge(z_lo_set, 2 * t + 2 + 4)
                    sp.sem_inc(sync_tick, 1)
                    sp.dma_start(out_lo[bass.ds(t * P, P), :], z[b]["lo"][:].bitcast(F32)).then_inc(z_stored[b], 16)

                by_twos(sp, step)
                for b in range(2):
                    sp.wait_ge(z_stored[b], 32 * (TILES // 2 + 1))

            @block.scalar
            def _(act):
                for k in range(KT):
                    act.wait_ge(w_in[k % 2], 16 * (k // 2 + 1))
                    nc.scalar.copy(w_part["hi"][:, k, :], w_land[k % 2][:]).then_inc(w_hi_set, 1)

                def x_hi(t, b):
                    act.wait_ge(turned, t + 1)
                    act.wait_ge(z_sum, 2 * t + 2)
                    for h in range(2):
                        cp = nc.scalar.copy(xt[b]["hi"][:, 4 * h:4 * h + 4, :], ps_x[h][:, :, 0:P])
                    cp.then_inc(xt_hi_set, 1)

                x_hi(0, 0)

                def step(i, b, last):
                    t = 2 * i + b
                    if not last:
                        x_hi(t + 1, 1 - b)
                    act.wait_ge(z_stored[b], 32 * i + 32)
                    for half in range(2):
                        cols = slice(half * BANK, (half + 1) * BANK)
                        if kind == "attention":
                            act.wait_ge(z_sum, 2 * t + half + 1 + 4)
                            nc.scalar.copy(z[b]["hi"][:, cols], ps_z[b][:, cols]).then_inc(z_hi_set, 1)
                        else:
                            act.wait_ge(mixed_set, 2 * t + half + 1)
                            act.sem_inc(act_tick, 1)
                            nc.scalar.activation(z[b]["hi"][:, cols], mixed[:, 0, cols], ACT.Copy,
                                                 scale=extra[1][:, bass.ds(t, 1)]).then_inc(z_hi_set, 1)

                by_twos(act, step)

            @block.vector
            def _(dve):
                dve.sem_inc(z_lo_set, 4)
                for k in range(KT):
                    dve.wait_ge(w_hi_set, k + 1)
                    nc.vector.tensor_tensor(w_part["lo"][:, k, :], w_land[k % 2][:],
                                            w_part["hi"][:, k, :].bitcast(F32), ALU.subtract).then_inc(w_lo_set, 1)
                dve.wait_ge(rows_in, 16 * len(row_list))

                def normalise(t, b):
                    nc.vector.tensor_scalar(xn[b][:], X[:, t, :], mean_var[:, t, 0:1], rstd[:, bass.ds(t, 1)],
                                            ALU.subtract, ALU.mult).then_inc(xn_set, 1)

                def x_lo(t, b):
                    dve.wait_ge(xt_hi_set, t + 1)
                    for h in range(2):
                        sub = nc.vector.tensor_tensor(xt[b]["lo"][:, 4 * h:4 * h + 4, :], ps_x[h][:, :, 0:P],
                                                      xt[b]["hi"][:, 4 * h:4 * h + 4, :].bitcast(F32), ALU.subtract)
                    sub.then_inc(xt_lo_set, 1)

                normalise(0, 0)
                x_lo(0, 0)
                normalise(1, 1)

                def step(i, b, last):
                    t = 2 * i + b
                    if not last:
                        x_lo(t + 1, 1 - b)
                    if not (isinstance(i, int) and i == TILES // 2 - 1):
                        dve.wait_ge(turned, t + 1)
                        normalise(t + 2, b)
                    dve.wait_ge(z_stored[b], 32 * i + 32)
                    for half in range(2):
                        cols = slice(half * BANK, (half + 1) * BANK)
                        if kind == "attention":
                            dve.wait_ge(z_hi_set, 2 * t + half + 1)
                            for side in range(2):
                                for h in (2 * half, 2 * half + 1):
                                    f = slice(h * HEAD_F, (h + 1) * HEAD_F)
                                    dot = nc.vector.tensor_tensor_reduce(mixed[:, side, f], ps_z[b][:, f], rows[:, side, f],
                                                                         1.0, 0.0, ALU.mult, ALU.add,
                                                                         dots[:, side, h:h + 1])
                            dot.then_inc(dots_set, 1)
                            nc.vector.tensor_tensor(z[b]["lo"][:, cols], ps_z[b][:, cols],
                                                    z[b]["hi"][:, cols].bitcast(F32), ALU.subtract).then_inc(z_lo_set, 1)
                        else:
                            dve.wait_ge(z_lo_set, 2 * t + half + 3)
                            dve.wait_ge(z_sum, 2 * t + half + 1 + 4)
                            nc.vector.tensor_tensor(mixed[:, 0, cols], ps_z[b][:, cols], rows[:, 0, cols],
                                                    ALU.add).then_inc(mixed_set, 1)
                            dve.wait_ge(z_hi_set, 2 * t + half + 1)
                            nc.vector.scalar_tensor_tensor(z[b]["lo"][:, cols], mixed[:, 0, cols], extra[1][:, bass.ds(t, 1)],
                                                           z[b]["hi"][:, cols].bitcast(F32), ALU.mult,
                                                           ALU.subtract).then_inc(z_lo_set, 1)
                    if kind == "attention":
                        dve.wait_ge(dots_set, 2 * t + 2)
                        nc.vector.tensor_copy(extra[2][:, t, :], dots[:, 0, :])
                        nc.vector.tensor_copy(extra[3][:, t, :], dots[:, 1, :]).then_inc(dots_out, 1)
                        dve.wait_ge(dots_out, t + 1)

                by_twos(dve, step)

            @block.tensor
            def _(pe):
                pe.sem_inc(z_sum, 4)

                def turn(t, b):
                    pe.wait_ge(xn_set, t + 1)
                    for k in range(KT):
                        mm = nc.tensor.transpose(ps_x[k // 4][:, k % 4, 0:P], xn[b][:, k * 128:(k + 1) * 128],
                                                 ident[0:P, 0:P])
                    mm.then_inc(turned, 1)

                turn(0, 0)
                pe.wait_ge(w_lo_set, KT)

                def step(i, b, last):
                    t = 2 * i + b
                    pe.wait_ge(xt_lo_set, t + 1)
                    if not last:
                        turn(t + 1, 1 - b)
                    for half in range(2):
                        pe.wait_ge(z_lo_set, 2 * t + half + 1)
                        cols = slice(half * BANK, (half + 1) * BANK)
                        for k in range(KT):
                            for n, (l, r) in enumerate(SPLIT):
                                mm = nc.tensor.matmul(ps_z[b][:, cols], xt[b][l][:, k, :], w_part[r][:, k, cols],
                                                      start=(k == 0 and n == 0), stop=(k == KT - 1 and n == 2))
                        mm.then_inc(z_sum, 1)

                by_twos(pe, step)


def attention(nc, X, ident, counts, counts_t, z_hi, z_lo, el, er, dis):
    HALF_T = TILES // 2
    HALF = HALF_T * P
    ZW = HEAD_F + 2
    STEPS = 4 * TILES
    with ExitStack() as ctx:
        c = Core(nc, ctx, "att")
        ct = c.sb("ct", [P, TILES, NODES], U16)
        row_a, row_b = c.sb("row_a", [P, HEADS, NODES], F32), c.sb("row_b", [P, HEADS, NODES], F32)
        zh = [{n: c.sb(f"zh_{n}{k}", [P, TILES, ZW], F32R) for n in ("hi", "lo")} for k in range(2)]
        cnt = [c.sb(f"cnt{k}", [P, NODES], U16) for k in range(2)]
        no_edge = [c.sb(f"no_edge{k}", [P, NODES], F32) for k in range(2)]
        junk = c.sb("junk", [P, HEADS, NODES], mybir.dt.bfloat16)
        max_el, top, peak = [c.sb(n, [P, TILES, HEADS], F32) for n in ("max_el", "top", "peak")]
        col_a, col_b, el_low = [c.sb(n, [P, TILES, HEADS], F32) for n in ("col_a", "col_b", "el_low")]
        low, arg, wexp, wt = [[c.sb(f"{n}{k}", [P, HALF], F32) for k in range(2)] for n in ("low", "arg", "wexp", "wt")]
        pt = [{n: c.sb(f"pt_{n}{k}", [P, HALF], F32R) for n in ("hi", "lo")} for k in range(2)]
        deg, root = c.sb("deg", [P, TILES], F32), c.sb("root", [P, TILES], F32)
        total, inv = c.sb("total", [P, HALF_T], F32), c.sb("inv", [P, HALF_T], F32)
        ct_in, cnt_in = c.sem("ct_in"), [c.sem(f"cnt_in{k}") for k in range(2)]
        z_in = [c.sem(f"z_in{k}") for k in range(2)]
        edgeless, maxed, cols_set = c.sem("edgeless"), c.sem("maxed"), c.sem("cols_set")
        pool_tick, sync_tick, max_out = c.sem("pool_tick"), c.sem("sync_tick"), c.sem("max_out")
        dve_tick = c.sem("dve_tick")
        tile_max = c.sb("tile_max", [P, HEADS], F32)
        rows_turned, rows_set = c.sem("rows_turned"), c.sem("rows_set")
        ones_set, deg_set, root_set, dis_set = c.sem("ones_set"), c.sem("deg_set"), c.sem("root_set"), c.sem("dis_set")

        with ExitStack() as inner:
            ci = Core(nc, inner, "rows")
            ps_row = [ci.ps(f"ps_row{k}", [128, 3, BANK]) for k in range(2)]
            with nc.Block() as block:

                @block.sync
                def _(sp):
                    for b in range(2):
                        sp.dma_start(cnt[b][:], counts[b * P:(b + 1) * P, :]).then_inc(cnt_in[b], 16)
                    sp.dma_start(ct[:], counts_t.rearrange("(t p) d -> p t d", p=P)).then_inc(ct_in, 16)
                    for b in range(2):
                        for n, d in (("hi", z_hi), ("lo", z_lo)):
                            sp.wait_ge(ones_set, 1)
                            sp.dma_start(zh[b][n][:, :, 0:HEAD_F].bitcast(F32),
                                         d.rearrange("(t p) (h f) -> p h t f", p=P, h=HEADS)[:, b]).then_inc(z_in[b], 16)
                    with sp.Fori(0, TILES // 2 - 1) as i:
                        for b in range(2):
                            sp.wait_ge(edgeless, 2 * i + b + 1)
                            sp.sem_inc(sync_tick, 1)
                            sp.dma_start(cnt[b][:], counts[bass.ds(i * (2 * P) + (b + 2) * P, P), :]).then_inc(cnt_in[b], 16)

                @block.gpsimd
                def _(pool):
                    for b in range(2):
                        for n, c0, value in (("hi", HEAD_F, 1.0), ("hi", HEAD_F + 1, 0.0), ("lo", HEAD_F, 0.0),
                                             ("lo", HEAD_F + 1, 0.0)):
                            ms = nc.gpsimd.memset(zh[b][n][:, :, c0:c0 + 1].bitcast(F32), value)
                    ms.then_inc(ones_set, 1)
                    pool.sem_inc(maxed, 2)
                    with pool.Fori(0, TILES // 2) as i:
                        for b in range(2):
                            pool.wait_ge(cnt_in[b], 16 * i + 16)
                            pool.wait_ge(maxed, 2 * i + b + 1)
                            pool.sem_inc(pool_tick, 1)
                            nc.gpsimd.tensor_scalar(no_edge[b][:], cnt[b][:], 0.0, FAR, ALU.is_equal,
                                                    ALU.mult).then_inc(edgeless, 1)

                @block.vector
                def _(dve):
                    nc.vector.tensor_scalar(el_low[:], el[:], SLOPE, None, ALU.mult)
                    dve.wait_ge(ct_in, 16)
                    nc.vector.tensor_reduce(deg[:], ct[:], AX.X, ALU.add).then_inc(deg_set, 1)
                    dve.wait_ge(rows_set, HEADS)
                    with dve.Fori(0, TILES // 2) as i:
                        for b in range(2):
                            dve.wait_ge(edgeless, 2 * i + b + 1)
                            dve.sem_inc(dve_tick, 1)
                            for h in range(HEADS):
                                mx = nc.vector.tensor_tensor_reduce(junk[:, h, :], no_edge[b][:], row_a[:, h, :], 1.0, FAR,
                                                                    ALU.add, ALU.max, tile_max[:, h:h + 1])
                            mx.then_inc(maxed, 1)
                            dve.wait_ge(maxed, 2 * i + b + 3)
                            nc.vector.tensor_copy(max_el[:, 2 * i + b, :], tile_max[:]).then_inc(max_out, 1)
                            dve.wait_ge(max_out, 2 * i + b + 1)
                    nc.vector.tensor_tensor(top[:], max_el[:], er[:], ALU.add).then_inc(cols_set, 1)
                    dve.wait_ge(cols_set, 1)
                    nc.vector.scalar_tensor_tensor(peak[:], top[:], SLOPE, top[:], ALU.mult, ALU.max).then_inc(cols_set, 1)
                    dve.wait_ge(cols_set, 2)
                    nc.vector.tensor_tensor(col_a[:], er[:], peak[:], ALU.subtract).then_inc(cols_set, 1)
                    nc.vector.scalar_tensor_tensor(col_b[:], er[:], SLOPE, peak[:], ALU.mult,
                                                   ALU.subtract).then_inc(cols_set, 1)
                    dve.wait_ge(root_set, 1)
                    nc.vector.reciprocal(dis[:], root[:]).then_inc(dis_set, 1)
                    dve.wait_ge(dis_set, 1)

                @block.scalar
                def _(act):
                    def take_rows(n, row, h):
                        act.wait_ge(rows_turned, n + 1)
                        for a, w in ((0, 4), (4, 4), (8, TILES - 8)):
                            cp = nc.scalar.copy(row[:, h, a * P:(a + w) * P], ps_row[n % 2][0:P, a // 4, 0:w * P])
                        cp.then_inc(rows_set, 1)

                    for h in range(HEADS):
                        take_rows(h, row_a, h)
                    act.wait_ge(deg_set, 1)
                    nc.scalar.activation(root[:], deg[:], ACT.Sqrt, bias=1.0).then_inc(root_set, 1)
                    for h in range(HEADS):
                        take_rows(HEADS + 2 * h, row_a, h)
                        take_rows(HEADS + 2 * h + 1, row_b, h)

                @block.tensor
                def _(pe):
                    def spread(n, col, h):
                        if n >= 2:
                            pe.wait_ge(rows_set, n - 1)
                        for t in range(TILES):
                            mm = nc.tensor.transpose(ps_row[n % 2][:, t // 4, (t % 4) * P:(t % 4 + 1) * P],
                                                     col[:, t, h:h + 1].broadcast_to((P, 128)), ident[0:P, 0:P])
                        mm.then_inc(rows_turned, 1)

                    for h in range(HEADS):
                        spread(h, el, h)
                    pe.wait_ge(cols_set, 4)
                    for h in range(HEADS):
                        spread(HEADS + 2 * h, col_a, h)
                        spread(HEADS + 2 * h + 1, col_b, h)

        low_set, arg_set, exp_set, wt_set = c.sem("low_set"), c.sem("arg_set"), c.sem("exp_set"), c.sem("wt_set")
        pt_hi_set, pt_lo_set, used = c.sem("pt_hi_set"), c.sem("pt_lo_set"), c.sem("pt_used")
        taken = c.sem("att_taken")
        inv_step = c.sem("inv_step")
        ps_o = c.ps("ps_o", [P, HALF_T, BANK])
        body = [(b, half, s) for b in range(2) for half in range(2) for s in range(TILES)]

        with nc.Block() as block:

            @block.sync
            def _(sp):
                with sp.Fori(0, 1) as i:
                    for b in range(2):
                        sp.wait_ge(taken, 2 * b + 3)
                        for n, d in (("hi", z_hi), ("lo", z_lo)):
                            sp.dma_start(zh[b][n][:, :, 0:HEAD_F].bitcast(F32),
                                         d.rearrange("(t p) (h f) -> p h t f", p=P, h=HEADS)[:, b + 2]).then_inc(z_in[b], 16)
                for b in range(2):
                    sp.wait_ge(z_in[b], 64)

            @block.gpsimd
            def _(pool):
                with pool.Fori(0, 2) as i:
                    for m, (b, half, s) in enumerate(body):
                        n = i * STEPS + m
                        pool.wait_ge(arg_set, n + 1)
                        pool.sem_inc(pool_tick, 1)
                        nc.gpsimd.tensor_tensor(low[m % 2][:], row_b[:, 2 * i + b, half * HALF:(half + 1) * HALF],
                                                el_low[:, s, bass.ds(2 * i + b, 1)].broadcast_to((P, HALF)),
                                                ALU.add).then_inc(low_set, 1)

            @block.vector
            def _(dve):
                dve.sem_inc(arg_set, 2)
                dve.sem_inc(wt_set, 2)
                dve.sem_inc(pt_lo_set, 2)
                dve.sem_inc(taken, 1)
                with dve.Fori(0, 2) as i:

                    def argument(m):
                        b, half, s = body[m]
                        n = i * STEPS + m
                        dve.wait_ge(low_set, n + 1)
                        dve.wait_ge(exp_set, n + 1)
                        nc.vector.scalar_tensor_tensor(arg[m % 2][:], row_a[:, 2 * i + b, half * HALF:(half + 1) * HALF],
                                                       el[:, s, bass.ds(2 * i + b, 1)], low[m % 2][:], ALU.add,
                                                       ALU.max).then_inc(arg_set, 1)

                    def weigh(m):
                        b, half, s = body[m]
                        dve.wait_ge(pt_lo_set, i * STEPS + m + 1)
                        dve.wait_ge(exp_set, i * STEPS + m + 3)
                        nc.vector.scalar_tensor_tensor(wt[m % 2][:], wexp[m % 2][:], 1.0,
                                                       ct[:, s, half * HALF:(half + 1) * HALF], ALU.min,
                                                       ALU.mult).then_inc(wt_set, 1)

                    def rest(m):
                        dve.wait_ge(pt_hi_set, i * STEPS + m + 1)
                        nc.vector.tensor_tensor(pt[m % 2]["lo"][:], wt[m % 2][:], pt[m % 2]["hi"][:].bitcast(F32),
                                                ALU.subtract).then_inc(pt_lo_set, 1)

                    def take(g):
                        b, half = g // 2, g % 2
                        dve.wait_ge(used, (i * 4 + g + 1) * TILES + 2)
                        nc.vector.tensor_scalar(total[:], ps_o[:, :, HEAD_F], 1e-30, None, ALU.max).then_inc(inv_step, 1)
                        dve.wait_ge(inv_step, (i * 4 + g) * 2 + 1)
                        nc.vector.reciprocal(inv[:], total[:]).then_inc(inv_step, 1)
                        dve.wait_ge(inv_step, (i * 4 + g) * 2 + 2)
                        for d in range(HALF_T):
                            to = X[:, half * HALF_T + d, bass.ds(i * (2 * HEAD_F) + b * HEAD_F, HEAD_F)]
                            st = nc.vector.scalar_tensor_tensor(to, ps_o[:, d, 0:HEAD_F], inv[:, d:d + 1], to,
                                                                ALU.mult, ALU.add)
                        st.then_inc(taken, 1)

                    for m in range(STEPS + 2):
                        if m < STEPS:
                            argument(m)
                        if 1 <= m <= STEPS:
                            weigh(m - 1)
                        if m >= 2:
                            rest(m - 2)
                        if m > TILES and (m - 2) % TILES == 0:
                            take((m - 2) // TILES - 1)
                    take(3)

            @block.scalar
            def _(act):
                act.sem_inc(exp_set, 2)
                with act.Fori(0, 2) as i:
                    for m in range(STEPS + 1):
                        n = i * STEPS + m
                        if m < STEPS:
                            act.wait_ge(arg_set, n + 3)
                            act.wait_ge(wt_set, n + 1)
                            nc.scalar.activation(wexp[m % 2][:], arg[m % 2][:], ACT.Exp).then_inc(exp_set, 1)
                        if m >= 1:
                            k = (m - 1) % 2
                            act.wait_ge(wt_set, n + 2)
                            act.wait_ge(used, n)
                            nc.scalar.copy(pt[k]["hi"][:], wt[k][:]).then_inc(pt_hi_set, 1)

            @block.tensor
            def _(pe):
                pe.sem_inc(used, 2)
                with pe.Fori(0, 2) as i:
                    for m, (b, half, s) in enumerate(body):
                        if half == 0 and s == 0:
                            pe.wait_ge(z_in[b], 32 * i + 32)
                        if s == 0:
                            pe.wait_ge(taken, i * 4 + m // TILES + 1)
                        pe.wait_ge(pt_lo_set, i * STEPS + m + 3)
                        for d in range(HALF_T):
                            for n, (l, r) in enumerate(SPLIT):
                                mm = nc.tensor.matmul(ps_o[:, d, 0:ZW], pt[m % 2][l][:, d * P:(d + 1) * P],
                                                      zh[b][r][:, s, :], start=(s == 0 and n == 0),
                                                      stop=(s == TILES - 1 and n == 2))
                        mm.then_inc(used, 1)


def rails(nc, X, mean_var, rstd, ident, maker, up, cproj):
    PARTS = TILES // 2
    W = 2 * P
    K4 = HEADS
    with ExitStack() as ctx:
        c = Core(nc, ctx, "rails")
        XN = c.sb("XN", [P, TILES, DIM], F32)
        mk, mk4 = c.sb("mk", [32, HEADS, 32], F32), c.sb("mk4", [32, HEADS, 4, 32], F32)
        upb = c.sb("upb", [32, HEADS, 128], F32)
        xcols = c.sb("xcols", [P, TILES, 4, 32], F32)
        tmp = [c.sb(f"tmp{k}", [128, BANK], F32R) for k in range(2)]
        xs = [c.sb(f"xs{k}", [128, NODES], F32R) for k in range(2)]
        cm = [c.sb(f"cm{k}", [128, HEADS, 128], F32R) for k in range(2)]
        minus_x, minus_c = c.sb("minus_x", [128, 1], F32), c.sb("minus_c", [128, 1], F32)
        act_f = [c.sb(f"act_f{k}", [128, HEADS, W], F32) for k in range(2)]
        hid = [{n: c.sb(f"hid_{n}{k}", [128, HEADS, W], F32R) for n in ("hi", "lo")} for k in range(2)]
        w_land = [c.sb(f"w_land{k}", [128, DIM], F32) for k in range(2)]
        w = [{n: c.sb(f"w_{n}{k}", [128, K4, DIM], F32R) for n in ("hi", "lo")} for k in range(2)]
        ps_prep = [c.ps(f"ps_prep{k}", [128, BANK]) for k in range(2)]
        ps_h = c.ps("ps_h", [128, 2, BANK])
        ps_acc = [c.ps(f"ps_acc{k}", [P, BANK]) for k in range(4)]
        zeros_set, masks_set, comb_in = c.sem("zeros_set"), c.sem("masks_set"), c.sem("comb_in")
        xn_set, mk4_set, xcols_set = c.sem("xn_set"), c.sem("mk4_set"), c.sem("xcols_set")
        prep_sum, prep_hi, prep_set = c.sem("prep_sum"), c.sem("prep_hi"), c.sem("prep_set")
        h_sum, gelu_set, hid_hi_set, hid_lo_set = c.sem("h_sum"), c.sem("gelu_set"), c.sem("hid_hi_set"), c.sem("hid_lo_set")
        w_in = [c.sem(f"w_in{k}") for k in range(2)]
        w_hi_set, w_lo_set = c.sem("w_hi_set"), c.sem("w_lo_set")
        acc_sum, acc_used = c.sem("acc_sum"), c.sem("acc_used")
        sync_tick, pool_tick = c.sem("sync_tick"), c.sem("pool_tick")
        groups = ((0, 4), (4, 8), (8, TILES))

        def over_pairs(eng, body):
            with eng.Fori(0, PAIRS // 2 - 1) as i:
                body(2 * i, 0, False)
                body(2 * i + 1, 1, False)
            body(PAIRS - 2, 0, False)
            body(PAIRS - 1, 1, True)

        with nc.Block() as block:

            @block.sync
            def _(sp):
                def comb_load(s):
                    for r in range(2):
                        sp.dma_start(mk[16 * r:16 * r + 16, :, 16 * r:16 * r + 16], maker[2 * s + r]).then_inc(comb_in, 16)
                        sp.dma_start(upb[16 * r:16 * r + 16, :, 64 * r:64 * r + 64], up[2 * s + r]).then_inc(comb_in, 16)

                def w_load(s, k):
                    sp.dma_start(w_land[k % 2][:], cproj[bass.ds(s * 128 + k * RAILS * RAIL_UP, 128), :])\
                      .then_inc(w_in[k % 2], 16)

                w_load(0, 0)
                w_load(0, 1)
                sp.wait_ge(zeros_set, 2)
                comb_load(0)

                def body(s, b, last):
                    for k in range(K4):
                        if last and k >= 2:
                            break
                        sp.wait_ge(w_lo_set, 4 * s + k + 1)
                        sp.sem_inc(sync_tick, 1)
                        w_load(s + k // 2, (k + 2) % 4)
                        if k == 1 and not last:
                            sp.wait_ge(prep_sum, 4 * s + 4)
                            sp.sem_inc(sync_tick, 1)
                            comb_load(s + 1)

                over_pairs(sp, body)

            @block.gpsimd
            def _(pool):
                nc.gpsimd.memset(mk[:], 0.0).then_inc(zeros_set, 1)
                nc.gpsimd.memset(upb[:], 0.0).then_inc(zeros_set, 1)

                def spread(s):
                    nc.gpsimd.tensor_copy(mk4[:], mk[:].unsqueeze(2).broadcast_to((32, HEADS, 4, 32))).then_inc(mk4_set, 1)
                    nc.gpsimd.tensor_copy(xcols[:], XN[:, :, bass.ds(s * 32, 32)].unsqueeze(2)
                                          .broadcast_to((P, TILES, 4, 32))).then_inc(xcols_set, 1)

                def hidden_hi(m, k):
                    pool.wait_ge(gelu_set, m + 2)
                    pool.wait_ge(acc_sum, 4 * m + 4)
                    pool.sem_inc(pool_tick, 1)
                    nc.gpsimd.tensor_copy(hid[k]["hi"][:], act_f[k][:]).then_inc(hid_hi_set, 1)

                pool.wait_ge(comb_in, 64)
                pool.wait_ge(xn_set, TILES)
                spread(0)
                hidden_hi(0, 0)

                def body(s, b, last):
                    if not last:
                        pool.wait_ge(comb_in, 64 * s + 128)
                        pool.wait_ge(prep_sum, 4 * s + 4)
                        pool.sem_inc(pool_tick, 1)
                        spread(s + 1)
                    for p in range(PARTS):
                        if not (last and p == PARTS - 1):
                            hidden_hi(PARTS * s + p + 1, (PARTS * b + p + 1) % 2)

                over_pairs(pool, body)

            @block.scalar
            def _(act):
                act.sem_inc(gelu_set, 1)

                def prep_round(s, g):
                    act.wait_ge(prep_sum, 4 * s + g + 1)
                    act.wait_ge(prep_set, 4 * s + g + 1)
                    n = BANK if g == 3 else (groups[g][1] - groups[g][0]) * P
                    nc.scalar.copy(tmp[g % 2][:, 0:n], ps_prep[g % 2][:, 0:n]).then_inc(prep_hi, 1)

                def w_round(s, k, b):
                    act.wait_ge(w_in[k % 2], 32 * s + (16 if k < 2 else 32))
                    nc.scalar.copy(w[b]["hi"][:, k, :], w_land[k % 2][:]).then_inc(w_hi_set, 1)

                def gelu(m, k):
                    act.wait_ge(h_sum, m + 1)
                    act.wait_ge(hid_lo_set, m + 1)
                    nc.scalar.activation(act_f[k][:].rearrange("p (a h) w -> p a (h w)", a=2), ps_h[:, :, 0:2 * W],
                                         ACT.Gelu).then_inc(gelu_set, 1)

                for k in range(K4):
                    w_round(0, k, 0)
                for g in range(4):
                    prep_round(0, g)
                gelu(0, 0)

                def body(s, b, last):
                    for p in range(PARTS):
                        if p < 4 and not last:
                            prep_round(s + 1, p)
                        if not (last and p == PARTS - 1):
                            gelu(PARTS * s + p + 1, (PARTS * b + p + 1) % 2)
                        if p < 4 and not last:
                            act.wait_ge(acc_sum, 20 * s + 8)
                            w_round(s + 1, p, 1 - b)

                over_pairs(act, body)

            @block.vector
            def _(dve):
                dve.sem_inc(prep_set, 2)
                dve.sem_inc(hid_lo_set, 2)
                dve.sem_inc(acc_used, 4)
                for q in range(4):
                    nc.vector.memset(minus_x[32 * q:32 * q + 32, :], -1.0 if q % 2 else 0.0).then_inc(masks_set, 1)
                    nc.vector.memset(minus_c[32 * q:32 * q + 32, :], -1.0 if q >= 2 else 0.0).then_inc(masks_set, 1)
                for t in range(TILES):
                    nc.vector.tensor_scalar(XN[:, t, :], X[:, t, :], mean_var[:, t, 0:1], rstd[:, t:t + 1],
                                            ALU.subtract, ALU.mult).then_inc(xn_set, 1)

                def prep_parts(s, g, b):
                    dve.wait_ge(prep_hi, 4 * s + g + 1)
                    if g < 3:
                        lo, hi = groups[g][0] * P, groups[g][1] * P
                        to, minus = xs[b][:, lo:hi], minus_x
                    else:
                        lo, hi = 0, BANK
                        to, minus = cm[b][:].rearrange("p h f -> p (h f)"), minus_c
                    nc.vector.scalar_tensor_tensor(to, tmp[g % 2][:, 0:hi - lo].bitcast(F32), minus[:, 0:1],
                                                   ps_prep[g % 2][:, 0:hi - lo], ALU.mult, ALU.add).then_inc(prep_set, 1)

                def w_rest(s, k, b):
                    dve.wait_ge(w_hi_set, 4 * s + k + 1)
                    nc.vector.tensor_tensor(w[b]["lo"][:, k, :], w_land[k % 2][:], w[b]["hi"][:, k, :].bitcast(F32),
                                            ALU.subtract).then_inc(w_lo_set, 1)

                def hidden_lo(m, k):
                    dve.wait_ge(hid_hi_set, m + 1)
                    nc.vector.tensor_tensor(hid[k]["lo"][:], act_f[k][:], hid[k]["hi"][:].bitcast(F32),
                                            ALU.subtract).then_inc(hid_lo_set, 1)

                for k in range(K4):
                    w_rest(0, k, 0)
                dve.wait_ge(masks_set, 8)
                for g in range(4):
                    prep_parts(0, g, 0)
                hidden_lo(0, 0)

                def body(s, b, last):
                    for p in range(PARTS):
                        m = PARTS * s + p
                        if p < 4 and not last:
                            dve.wait_ge(gelu_set, PARTS * s + 1)
                            prep_parts(s + 1, p, 1 - b)
                        if not (last and p == PARTS - 1):
                            hidden_lo(m + 1, (PARTS * b + p + 1) % 2)
                        if p < 4 and not last:
                            w_rest(s + 1, p, 1 - b)
                        for j in range(4):
                            dve.wait_ge(acc_sum, 4 * m + j + 9)
                            to = X[:, 2 * p + j // 2, (j % 2) * BANK:(j % 2 + 1) * BANK]
                            nc.vector.tensor_tensor(to, ps_acc[j][:], to, ALU.add).then_inc(acc_used, 1)

                over_pairs(dve, body)

            @block.tensor
            def _(pe):
                pe.sem_inc(acc_sum, 8)

                def prepare(s, g):
                    pe.wait_ge(prep_set, 4 * s + g + 1)
                    if g < 3:
                        pe.wait_ge(xcols_set, s + 1)
                        lo, hi = groups[g]
                        for t in range(lo, hi):
                            mm = nc.tensor.transpose(ps_prep[g % 2][:, (t - lo) * P:(t - lo + 1) * P],
                                                     xcols[:, t].rearrange("p q f -> p (q f)"), ident[0:P, 0:P])
                    else:
                        pe.wait_ge(mk4_set, s + 1)
                        for h in range(HEADS):
                            mm = nc.tensor.matmul(ps_prep[1][:, h * 128:(h + 1) * 128],
                                                  mk4[:, h].rearrange("p q f -> p (q f)"), upb[:, h, :],
                                                  start=True, stop=True)
                    mm.then_inc(prep_sum, 1)

                def hidden(s, p, b):
                    if p == 0:
                        pe.wait_ge(prep_set, 4 * s + 6)
                    pe.wait_ge(gelu_set, PARTS * s + p + 1)
                    for h in range(HEADS):
                        mm = nc.tensor.matmul(ps_h[:, h // 2, (h % 2) * W:(h % 2 + 1) * W], cm[b][:, h, :],
                                              xs[b][:, p * W:(p + 1) * W], start=True, stop=True)
                    mm.then_inc(h_sum, 1)

                def project(s, p, b):
                    m, k2 = PARTS * s + p, (PARTS * b + p) % 2
                    if p == 0:
                        pe.wait_ge(w_lo_set, 4 * s + 4)
                    pe.wait_ge(hid_lo_set, m + 3)
                    for j in range(4):
                        pe.wait_ge(acc_used, 4 * m + j + 1)
                        cols = slice((j % 2) * BANK, (j % 2 + 1) * BANK)
                        for k in range(K4):
                            for n, (l, r) in enumerate(SPLIT):
                                mm = nc.tensor.matmul(ps_acc[j][:], hid[k2][l][:, k, (j // 2) * P:(j // 2 + 1) * P],
                                                      w[b][r][:, k, cols], start=(k == 0 and n == 0),
                                                      stop=(k == K4 - 1 and n == 2))
                        mm.then_inc(acc_sum, 1)

                for g in range(4):
                    prepare(0, g)
                hidden(0, 0, 0)

                def body(s, b, last):
                    for p in range(PARTS):
                        if p < 4 and not last:
                            prepare(s + 1, p)
                        if p < PARTS - 1:
                            hidden(s, p + 1, b)
                        elif not last:
                            hidden(s + 1, 0, 1 - b)
                        project(s, p, b)

                over_pairs(pe, body)


def aggregate(nc, X, ident, counts, h_hi, h_lo, dis):
    with ExitStack() as ctx:
        c = Core(nc, ctx, "agg")
        cnt = c.sb("cnt", [P, TILES, NODES], U16)
        h = {n: c.sb(f"h_{n}", [P, TILES, DIM], F32R) for n in ("hi", "lo")}
        cf = [c.sb(f"cf{k}", [P, TILES, P], F32) for k in range(2)]
        cp = [{n: c.sb(f"c_{n}{k}", [P, TILES, P], F32R) for n in ("hi", "lo")} for k in range(2)]
        ps_o = [c.ps(f"ps_o{k}", [P, 2 * BANK]) for k in range(2)]
        cnt_in, h_in = c.sem("cnt_in"), [c.sem(f"h_in{t}") for t in range(TILES)]
        cf_set, self_set, hi_set, lo_set = c.sem("cf_set"), c.sem("self_set"), c.sem("hi_set"), c.sem("lo_set")
        summed, added, dve_tick = c.sem("summed"), c.sem("added"), c.sem("dve_tick")

        with nc.Block() as block:

            @block.sync
            def _(sp):
                sp.dma_start(cnt[:], counts.rearrange("(t p) s -> p t s", p=P)).then_inc(cnt_in, 16)
                for t in range(TILES):
                    for n, d in (("hi", h_hi), ("lo", h_lo)):
                        sp.dma_start(h[n][:, t, :].bitcast(F32), d[t * P:(t + 1) * P, :]).then_inc(h_in[t], 16)

            @block.vector
            def _(dve):
                dve.sem_inc(lo_set, 2)
                dve.sem_inc(added, 4)
                dve.wait_ge(cnt_in, 16)

                def matrix(j, b):
                    dve.wait_ge(lo_set, j + 1)
                    dve.sem_inc(dve_tick, 1)
                    nc.vector.tensor_copy(cf[b][:], cnt[:, :, bass.ds(j * P, P)]).then_inc(cf_set, 1)
                    dve.wait_ge(cf_set, j + 1)
                    nc.vector.tensor_tensor(cf[b][:, j, :], cf[b][:, j, :], ident[0:P, 0:P], ALU.add).then_inc(self_set, 1)
                    dve.wait_ge(hi_set, j + 1)
                    nc.vector.tensor_tensor(cp[b]["lo"][:], cf[b][:], cp[b]["hi"][:].bitcast(F32),
                                            ALU.subtract).then_inc(lo_set, 1)

                matrix(0, 0)

                def step(i, b, last):
                    j = 2 * i + b
                    if not last:
                        matrix(j + 1, 1 - b)
                    for half in range(2):
                        cols = slice(half * BANK, (half + 1) * BANK)
                        dve.wait_ge(summed, 2 * j + half + 5)
                        nc.vector.scalar_tensor_tensor(X[:, j, cols], ps_o[b][:, cols], dis[:, bass.ds(j, 1)],
                                                       X[:, j, cols], ALU.mult, ALU.add).then_inc(added, 1)

                by_twos(dve, step)

            @block.scalar
            def _(act):
                def step(i, b, last):
                    j = 2 * i + b
                    act.wait_ge(self_set, j + 1)
                    act.wait_ge(summed, 2 * j + 2)
                    nc.scalar.copy(cp[b]["hi"][:], cf[b][:]).then_inc(hi_set, 1)

                by_twos(act, step)

            @block.tensor
            def _(pe):
                pe.sem_inc(summed, 4)
                for t in range(TILES):
                    pe.wait_ge(h_in[t], 32)

                def step(i, b, last):
                    j = 2 * i + b
                    pe.wait_ge(lo_set, j + 3)
                    for half in range(2):
                        cols = slice(half * BANK, (half + 1) * BANK)
                        pe.wait_ge(added, 2 * j + half + 1)
                        for t in range(TILES):
                            for n, (l, r) in enumerate(SPLIT):
                                mm = nc.tensor.matmul(ps_o[b][:, cols], cp[b][l][:, t, :], h[r][:, t, cols],
                                                      start=(t == 0 and n == 0), stop=(t == TILES - 1 and n == 2))
                        mm.then_inc(summed, 1)

                by_twos(pe, step)


def tiles_of(eng, n, step):
    pairs = (n - 3) // 2
    step(0, 0, 3)
    step(1, 1, 3)
    with eng.Fori(1, pairs) as i:
        step(2 * i, 0, 3)
        step(2 * i + 1, 1, 3)
    for t in range(2 * pairs, n):
        step(t, t % 2, min(n - 1 - t, 3))


class Expert:

    def __init__(self, c, rows, weights):
        self.rows = rows
        self.x = [c.sb(f"x{k}", [rows, DIM], F32) for k in range(2)]
        self.xt = [{n: c.sb(f"xt_{n}{k}", [128, KT, rows], F32R) for n in ("hi", "lo")} for k in range(2)]
        self.w12 = [{n: c.sb(f"w12_{n}{k}", [128, KT, 2 * INTER], F32R) for n in ("hi", "lo")} for k in range(weights)]
        self.w3 = [{n: c.sb(f"w3_{n}{k}", [128, 2, DIM], F32R) for n in ("hi", "lo")} for k in range(weights)]
        self.land = [c.sb(f"w_land{k}", [128, 2048], F32) for k in range(3)]
        self.gelu = [c.sb(f"gelu{k}", [rows, INTER], F32) for k in range(2)]
        self.gate = [c.sb(f"gate{k}", [rows, INTER], F32) for k in range(2)]
        self.gt = {n: c.sb(f"gt_{n}", [128, 2, rows], F32R) for n in ("hi", "lo")}
        self.ps_x = [c.ps(f"ps_x{k}", [128, 4, 128]) for k in range(2)]
        self.ps_ab = [c.ps(f"ps_ab{k}", [rows, BANK]) for k in range(2)]
        self.ps_g = c.ps("ps_g", [128, 2, 128])
        self.ps_y = c.ps("ps_y", [rows, 2 * BANK])
        self.x_set = c.sem("x_set")
        self.turned = c.sem("turned")
        self.xt_hi_set = c.sem("xt_hi_set")
        self.xt_lo_set = c.sem("xt_lo_set")
        self.up_sum = c.sem("up_sum")
        self.gelu_set = c.sem("gelu_set")
        self.gate_set = c.sem("gate_set")
        self.g_turned = c.sem("g_turned")
        self.gt_hi_set = c.sem("gt_hi_set")
        self.gt_lo_set = c.sem("gt_lo_set")
        self.y_sum = c.sem("y_sum")
        self.y_taken = c.sem("y_taken")
        self.land_in = [c.sem(f"land_in{k}") for k in range(3)]
        self.split_hi = [c.sem(f"split_hi{k}") for k in range(3)]
        self.split_lo = [c.sem(f"split_lo{k}") for k in range(3)]
        self.act_tick, self.dve_tick = c.sem("act_tick"), c.sem("dve_tick")
        self.pool_tick, self.sync_tick = c.sem("pool_tick"), c.sem("sync_tick")

    def piece(self, k, part, n):
        if n == 2:
            return self.w3[k][part][:]
        return self.w12[k][part][:, :, n * INTER:(n + 1) * INTER]

    def landed(self, n):
        return self.land[n][:].rearrange("p (k f) -> p k f", k=2 if n == 2 else KT)


def shared_expert(nc, X, mean_var, rstd, ident, w1, w2, w3, wg, xn_out, logits):
    with ExitStack() as ctx:
        c = Core(nc, ctx, "shared")
        e = Expert(c, P, 1)
        wg_f = c.sb("wg_f", [128, KT, EXPERTS], F32)
        wg_part = {n: c.sb(f"wg_{n}", [128, KT, EXPERTS], F32R) for n in ("hi", "lo")}
        ps_l = c.ps("ps_l", [P, EXPERTS])
        wg_in, wg_hi_set, wg_lo_set = c.sem("wg_in"), c.sem("wg_hi_set"), c.sem("wg_lo_set")
        logits_sum, logits_set = c.sem("logits_sum"), c.sem("logits_set")
        x_stored = [c.sem(f"x_stored{k}") for k in range(2)]
        with nc.Block() as block:

            @block.sync
            def _(sp):
                for n, w in enumerate((w1, w2, w3)):
                    sp.dma_start(e.landed(n), w.rearrange("(k p) f -> p k f", p=128)).then_inc(e.land_in[n], 16)
                sp.dma_start(wg_f[:], wg.rearrange("(k p) f -> p k f", p=128)).then_inc(wg_in, 16)
                for b in range(2):
                    sp.sem_inc(x_stored[b], 16)

                def store(t, b):
                    sp.wait_ge(e.x_set, t + 1)
                    sp.sem_inc(e.sync_tick, 1)
                    sp.dma_start(xn_out[bass.ds(t * P, P), :], e.x[b][:]).then_inc(x_stored[b], 16)

                tiles_of(sp, TILES, lambda t, b, left: store(t, b))
                for b in range(2):
                    sp.wait_ge(x_stored[b], 16 * (TILES // 2 + 1))

            @block.scalar
            def _(act):
                act.wait_ge(wg_in, 16)
                nc.scalar.copy(wg_part["hi"][:], wg_f[:]).then_inc(wg_hi_set, 1)
                for n in range(3):
                    act.wait_ge(e.land_in[n], 16)
                    nc.scalar.copy(e.piece(0, "hi", n), e.landed(n)).then_inc(e.split_hi[n], 1)

                def x_hi(t, b):
                    act.wait_ge(e.turned, t + 1)
                    act.wait_ge(e.up_sum, t + 1)
                    for h in range(2):
                        cp = nc.scalar.copy(e.xt[b]["hi"][:, 4 * h:4 * h + 4, :], e.ps_x[h][:, :, 0:P])
                    cp.then_inc(e.xt_hi_set, 1)

                def gelu(t, b):
                    act.wait_ge(e.up_sum, t + 3)
                    act.wait_ge(e.gate_set, t + 1)
                    nc.scalar.activation(e.gelu[b][:], e.ps_ab[b][:, 0:INTER], ACT.Gelu).then_inc(e.gelu_set, 1)

                x_hi(0, 0)
                gelu(0, 0)
                x_hi(1, 1)

                def step(t, b, left):
                    act.wait_ge(e.g_turned, t + 1)
                    act.wait_ge(e.y_sum, t + 1)
                    nc.scalar.copy(e.gt["hi"][:], e.ps_g[:, :, 0:P]).then_inc(e.gt_hi_set, 1)
                    if left >= 1:
                        gelu(t + 1, 1 - b)
                    if left >= 2:
                        x_hi(t + 2, b)

                tiles_of(act, TILES, step)

            @block.vector
            def _(dve):
                dve.sem_inc(e.gate_set, 2)
                dve.sem_inc(e.y_taken, 1)

                def normalise(t, b):
                    if not isinstance(t, int) or t >= 2:
                        dve.wait_ge(e.turned, t - 1)
                    dve.wait_ge(x_stored[b], 8 * t - 8 * b + 16)
                    nc.vector.tensor_scalar(e.x[b][:], X[:, t, :], mean_var[:, t, 0:1], rstd[:, bass.ds(t, 1)],
                                            ALU.subtract, ALU.mult).then_inc(e.x_set, 1)

                def x_lo(t, b):
                    dve.wait_ge(e.xt_hi_set, t + 1)
                    for h in range(2):
                        sub = nc.vector.tensor_tensor(e.xt[b]["lo"][:, 4 * h:4 * h + 4, :], e.ps_x[h][:, :, 0:P],
                                                      e.xt[b]["hi"][:, 4 * h:4 * h + 4, :].bitcast(F32), ALU.subtract)
                    sub.then_inc(e.xt_lo_set, 1)

                def gate(t, b):
                    dve.wait_ge(e.gelu_set, t + 1)
                    if not isinstance(t, int) or t >= 2:
                        dve.wait_ge(e.g_turned, t - 1)
                    nc.vector.tensor_tensor(e.gate[b][:], e.gelu[b][:], e.ps_ab[b][:, INTER:2 * INTER],
                                            ALU.mult).then_inc(e.gate_set, 1)
                    dve.wait_ge(logits_sum, t + 1)
                    dve.sem_inc(e.dve_tick, 1)
                    nc.vector.tensor_copy(logits[:, t, :], ps_l[:]).then_inc(logits_set, 1)

                normalise(0, 0)
                normalise(1, 1)
                dve.wait_ge(wg_hi_set, 1)
                nc.vector.tensor_tensor(wg_part["lo"][:], wg_f[:], wg_part["hi"][:].bitcast(F32),
                                        ALU.subtract).then_inc(wg_lo_set, 1)
                x_lo(0, 0)
                normalise(2, 0)
                for n in range(3):
                    dve.wait_ge(e.split_hi[n], 1)
                    nc.vector.tensor_tensor(e.piece(0, "lo", n), e.landed(n), e.piece(0, "hi", n).bitcast(F32),
                                            ALU.subtract).then_inc(e.split_lo[n], 1)
                gate(0, 0)
                x_lo(1, 1)

                def step(t, b, left):
                    dve.wait_ge(e.gt_hi_set, t + 1)
                    nc.vector.tensor_tensor(e.gt["lo"][:], e.ps_g[:, :, 0:P], e.gt["hi"][:].bitcast(F32),
                                            ALU.subtract).then_inc(e.gt_lo_set, 1)
                    if left >= 3:
                        normalise(t + 3, 1 - b)
                    if left >= 1:
                        gate(t + 1, 1 - b)
                    if left >= 2:
                        x_lo(t + 2, b)
                    dve.wait_ge(e.y_sum, t + 2)
                    nc.vector.tensor_tensor(X[:, t, :], e.ps_y[:], X[:, t, :], ALU.add).then_inc(e.y_taken, 1)

                tiles_of(dve, TILES, step)

            @block.tensor
            def _(pe):
                pe.sem_inc(e.up_sum, 2)
                pe.sem_inc(e.y_sum, 1)

                def turn(t, b):
                    pe.wait_ge(e.x_set, t + 1)
                    if not isinstance(t, int) or t >= 1:
                        pe.wait_ge(e.xt_lo_set, t)
                    for k in range(KT):
                        mm = nc.tensor.transpose(e.ps_x[k // 4][:, k % 4, 0:P], e.x[b][:, k * 128:(k + 1) * 128],
                                                 ident[0:P, 0:P])
                    mm.then_inc(e.turned, 1)

                def up(t, b):
                    pe.wait_ge(e.xt_lo_set, t + 1)
                    pe.wait_ge(e.gate_set, t + 1)
                    if isinstance(t, int) and t == 0:
                        pe.wait_ge(wg_lo_set, 1)
                    else:
                        pe.wait_ge(logits_set, t)
                    for k in range(KT):
                        for n, (l, r) in enumerate(SPLIT):
                            mm = nc.tensor.matmul(ps_l[:], e.xt[b][l][:, k, :], wg_part[r][:, k, :],
                                                  start=(k == 0 and n == 0), stop=(k == KT - 1 and n == 2))
                    mm.then_inc(logits_sum, 1)
                    if isinstance(t, int) and t == 0:
                        pe.wait_ge(e.split_lo[0], 1)
                        pe.wait_ge(e.split_lo[1], 1)
                    for k in range(KT):
                        for n, (l, r) in enumerate(SPLIT):
                            mm = nc.tensor.matmul(e.ps_ab[b][:], e.xt[b][l][:, k, :], e.w12[0][r][:, k, :],
                                                  start=(k == 0 and n == 0), stop=(k == KT - 1 and n == 2))
                    mm.then_inc(e.up_sum, 1)

                def down(t):
                    pe.wait_ge(e.gt_lo_set, t + 1)
                    pe.wait_ge(e.y_taken, t + 1)
                    for half in range(2):
                        cols = slice(half * BANK, (half + 1) * BANK)
                        for k in range(2):
                            for n, (l, r) in enumerate(SPLIT):
                                mm = nc.tensor.matmul(e.ps_y[:, cols], e.gt[l][:, k, :], e.w3[0][r][:, k, cols],
                                                      start=(k == 0 and n == 0), stop=(k == 1 and n == 2))
                    mm.then_inc(e.y_sum, 1)

                turn(0, 0)
                up(0, 0)
                turn(1, 1)
                pe.wait_ge(e.split_lo[2], 1)

                def step(t, b, left):
                    pe.wait_ge(e.gate_set, t + 3)
                    if not isinstance(t, int) or t >= 1:
                        pe.wait_ge(e.gt_lo_set, t)
                    for k in range(2):
                        mm = nc.tensor.transpose(e.ps_g[:, k, 0:P], e.gate[b][:, k * 128:(k + 1) * 128], ident[0:P, 0:P])
                    mm.then_inc(e.g_turned, 1)
                    if left >= 1:
                        up(t + 1, 1 - b)
                    if left >= 2:
                        turn(t + 2, b)
                    down(t)

                tiles_of(pe, TILES, step)


def route(nc, logits, ident, tokens_d, tokens, slot_expert):
    with ExitStack() as ctx:
        c = Core(nc, ctx, "route")
        TE = [P, TILES, EXPERTS]
        best, best_key = c.sb("best", [P, TILES], F32), c.sb("best_key", [P, TILES], F32)
        rank_i, rank = c.sb("rank_i", TE, I32), c.sb("rank", TE, F32)
        is_best, key, hot = c.sb("is_best", TE, F32), c.sb("key", TE, F32), c.sb("hot", TE, F32)
        upper, ones = c.sb("upper", [P, P], F32), c.sb("ones", [P, P], F32)
        cum = c.sb("cum", [P, TILES + 1, EXPERTS], F32)
        level_i, level = c.sb("level_i", [P, EXPERTS, TILES], I32), c.sb("level", [P, EXPERTS, TILES], F32)
        above = c.sb("above", [P, EXPERTS, TILES], F32)
        slots, upto, base = [c.sb(n, [P, EXPERTS], F32) for n in ("slots", "upto", "base")]
        order_i, order = c.sb("order_i", [P, EXPERTS, EXPERTS], I32), c.sb("order", [P, EXPERTS, EXPERTS], F32)
        counted = c.sb("counted", [P, EXPERTS, EXPERTS], F32)
        place1, place2, place3 = c.sb("place1", TE, F32), c.sb("place2", TE, F32), c.sb("place3", TE, F32)
        pos, pos_i = c.sb("pos", [P, TILES], F32), c.sb("pos_i", [P, TILES], I32)
        slot_i, slot = c.sb("slot_i", [1, SLOTS, EXPERTS], I32), c.sb("slot", [1, SLOTS, EXPERTS], F32)
        past = c.sb("past", [1, SLOTS, EXPERTS], F32)
        of_slot = c.sb("of_slot", [1, SLOTS], F32)
        node = c.sb("node", [P, TILES], I32)
        nobody = c.sb("nobody", [SLOT, SLOTS], I32)
        ps_rank, ps_all = c.ps("ps_rank", TE), c.ps("ps_all", TE)
        made, step, hot_set, ranked = c.sem("made"), c.sem("step"), c.sem("hot_set"), c.sem("ranked")
        pos_set, filled, sent, back = c.sem("pos_set"), c.sem("filled"), c.sem("sent"), c.sem("back")
        upper_set = c.sem("upper_set")
        with nc.Block() as block:

            @block.gpsimd
            def _(pool):
                nc.gpsimd.iota(nobody[:], [[0, SLOTS]], base=2 * NODES, channel_multiplier=0).then_inc(made, 1)
                nc.gpsimd.iota(rank_i[:], [[0, TILES], [-1, EXPERTS]], base=EXPERTS, channel_multiplier=0).then_inc(made, 1)
                nc.gpsimd.iota(level_i[:], [[0, EXPERTS], [SLOT, TILES]], base=0, channel_multiplier=0).then_inc(made, 1)
                nc.gpsimd.iota(order_i[:], [[-1, EXPERTS], [1, EXPERTS]], base=0, channel_multiplier=0).then_inc(made, 1)
                nc.gpsimd.iota(slot_i[:], [[1, SLOTS], [0, EXPERTS]], base=0, channel_multiplier=0).then_inc(made, 1)
                nc.gpsimd.iota(node[:], [[P, TILES]], base=0, channel_multiplier=1).then_inc(made, 1)
                nc.gpsimd.memset(ones[:], 1.0).then_inc(made, 1)
                pool.wait_ge(made, 7)
                nc.gpsimd.affine_select(out=upper[:], in_=ones[:], compare_op=ALU.is_gt, fill=0.0, base=0,
                                        pattern=[[1, P]], channel_multiplier=-1).then_inc(upper_set, 1)
                pool.wait_ge(pos_set, 1)
                pool.wait_ge(filled, 16)
                for t in range(TILES):
                    nc.gpsimd.indirect_dma_start(out=tokens_d, out_offset=bass.IndirectOffsetOnAxis(ap=pos_i[:, t:t + 1], axis=0),
                                                 in_=node[:, t:t + 1], in_offset=None).then_inc(sent, 16)

            @block.sync
            def _(sp):
                sp.wait_ge(made, 1)
                sp.dma_start(tokens_d.rearrange("(p j) a -> p (j a)", p=SLOT), nobody[:]).then_inc(filled, 16)
                sp.wait_ge(sent, 16 * TILES)
                sp.dma_start(tokens[:], tokens_d.rearrange("(j p) a -> p (j a)", p=SLOT),
                             allow_slow_non_contiguous=True).then_inc(back, 16)
                sp.wait_ge(back, 16)

            @block.vector
            def _(dve):
                n = [0]

                def chain(ins):
                    n[0] += 1
                    ins.then_inc(step, 1)
                    dve.wait_ge(step, n[0])

                def bc(a, shape, axis):
                    return a.unsqueeze(axis).broadcast_to(shape)

                dve.wait_ge(made, 7)
                for a, b in ((rank, rank_i), (level, level_i), (order, order_i)):
                    nc.vector.tensor_copy(a[:], b[:])
                nc.vector.tensor_copy(slot[:], slot_i[:])
                chain(nc.vector.tensor_reduce(best[:], logits[:], AX.X, ALU.max))
                chain(nc.vector.tensor_tensor(is_best[:], logits[:], bc(best[:], TE, 2), ALU.is_equal))
                chain(nc.vector.tensor_tensor(key[:], is_best[:], rank[:], ALU.mult))
                chain(nc.vector.tensor_reduce(best_key[:], key[:], AX.X, ALU.max))
                nc.vector.tensor_tensor(hot[:], key[:], bc(best_key[:], TE, 2), ALU.is_equal).then_inc(hot_set, 1)
                chain(nc.vector.memset(cum[:, 0, :], 0.0))
                dve.wait_ge(ranked, 1)
                for t in range(TILES):
                    chain(nc.vector.tensor_tensor(cum[:, t + 1, :], cum[:, t, :], ps_all[:, t, :], ALU.add))
                chain(nc.vector.tensor_tensor(above[:], level[:], bc(cum[:, TILES, :], [P, EXPERTS, TILES], 2), ALU.is_lt))
                chain(nc.vector.tensor_reduce(slots[:], above[:], AX.X, ALU.add))
                chain(nc.vector.scalar_tensor_tensor(counted[:], order[:], 0.0, bc(slots[:], [P, EXPERTS, EXPERTS], 1),
                                                     ALU.is_le, ALU.mult))
                chain(nc.vector.tensor_reduce(upto[:], counted[:], AX.X, ALU.add))
                chain(nc.vector.tensor_tensor(base[:], upto[:], slots[:], ALU.subtract))
                chain(nc.vector.tensor_tensor(place1[:], cum[:, 0:TILES, :], ps_rank[:], ALU.add))
                chain(nc.vector.scalar_tensor_tensor(place2[:], bc(base[:], TE, 1), float(SLOT), place1[:], ALU.mult, ALU.add))
                chain(nc.vector.tensor_tensor(place3[:], place2[:], hot[:], ALU.mult))
                chain(nc.vector.tensor_reduce(pos[:], place3[:], AX.X, ALU.add))
                nc.vector.tensor_copy(pos_i[:], pos[:]).then_inc(pos_set, 1)
                chain(nc.vector.tensor_tensor(past[:], slot[:], bc(upto[0:1, :], [1, SLOTS, EXPERTS], 1), ALU.is_ge))
                chain(nc.vector.tensor_reduce(of_slot[:], past[:], AX.X, ALU.add))
                chain(nc.vector.tensor_scalar(slot_expert[:], of_slot[:], float(EXPERTS - 1), None, ALU.min))

            @block.tensor
            def _(pe):
                pe.wait_ge(hot_set, 1)
                pe.wait_ge(upper_set, 1)
                flat = hot[:].rearrange("p t e -> p (t e)")
                nc.tensor.matmul(ps_rank[:].rearrange("p t e -> p (t e)"), upper[:], flat, start=True, stop=True)
                nc.tensor.matmul(ps_all[:].rearrange("p t e -> p (t e)"), ones[:], flat, start=True,
                                 stop=True).then_inc(ranked, 1)


def routed_experts(nc, ident, W1, W2, W3, xn_d, y_d, tokens, slot_expert):
    with ExitStack() as ctx:
        c = Core(nc, ctx, "routed")
        e = Expert(c, SLOT, 2)
        y = [c.sb(f"y{k}", [SLOT, DIM], F32) for k in range(2)]
        who_in = [c.sb(f"who_in{k}", [SLOT, 1], I32) for k in range(2)]
        who_out = [c.sb(f"who_out{k}", [SLOT, 1], I32) for k in range(2)]
        zeroed, who_set, who_out_set = c.sem("zeroed"), c.sem("who_set"), c.sem("who_out_set")
        x_in = [c.sem(f"x_in{k}") for k in range(2)]
        y_set, y_stored = c.sem("y_set"), [c.sem(f"y_stored{k}") for k in range(2)]
        sources = [w.rearrange("e (k p) f -> e p k f", p=128) for w in (W1, W2, W3)]
        with nc.Block() as block:

            @block.sync
            def _(sp):
                def load(t, n):
                    if not isinstance(t, int) or t >= 1:
                        sp.wait_ge(e.split_lo[n], t)
                        sp.sem_inc(e.sync_tick, 1)
                    which = sp.value_load(slot_expert[0:1, bass.ds(t, 1)], min_val=0, max_val=EXPERTS - 1)
                    sp.dma_start(e.landed(n), sources[n][which]).then_inc(e.land_in[n], 16)

                for n in range(3):
                    load(0, n)
                with sp.Fori(1, SLOTS) as t:
                    for n in range(3):
                        load(t, n)

            @block.gpsimd
            def _(pool):
                for b in range(2):
                    nc.gpsimd.memset(e.x[b][:], 0.0).then_inc(zeroed, 1)
                pool.wait_ge(zeroed, 2)

                def gather(t, b):
                    if not isinstance(t, int) or t >= 2:
                        pool.wait_ge(e.turned, t - 1)
                        pool.wait_ge(x_in[b], 8 * t - 8 * b)
                    pool.sem_inc(e.pool_tick, 1)
                    nc.gpsimd.tensor_copy(who_in[b][:], tokens[:, bass.ds(t, 1)]).then_inc(who_set, 1)
                    pool.wait_ge(who_set, t + 1)
                    pool.sem_inc(e.pool_tick, 1)
                    nc.gpsimd.indirect_dma_start(out=e.x[b][:], out_offset=None, in_=xn_d,
                                                 in_offset=bass.IndirectOffsetOnAxis(ap=who_in[b][:], axis=0),
                                                 bounds_check=NODES - 1, oob_is_err=False).then_inc(x_in[b], 16)

                def split(t, b, n, low):
                    pool.wait_ge(e.land_in[n], 16 * t + 16)
                    if not isinstance(t, int) or t >= 2:
                        pool.wait_ge(e.y_sum if n == 2 else e.up_sum, t if n == 2 else t + 1)
                    pool.sem_inc(e.pool_tick, 1)
                    nc.gpsimd.tensor_copy(e.piece(b, "hi", n), e.landed(n)).then_inc(e.split_hi[n], 1)
                    if low:
                        pool.wait_ge(e.split_hi[n], t + 1)
                        pool.sem_inc(e.pool_tick, 1)
                        nc.gpsimd.tensor_tensor(e.piece(b, "lo", n), e.landed(n), e.piece(b, "hi", n).bitcast(F32),
                                                ALU.subtract).then_inc(e.split_lo[n], 1)

                def scatter(t, b):
                    if not isinstance(t, int) or t >= 2:
                        pool.wait_ge(y_stored[b], 8 * t - 8 * b)
                    pool.sem_inc(e.pool_tick, 1)
                    nc.gpsimd.tensor_copy(who_out[b][:], tokens[:, bass.ds(t, 1)]).then_inc(who_out_set, 1)
                    pool.wait_ge(who_out_set, t + 1)
                    pool.wait_ge(y_set, t + 1)
                    pool.sem_inc(e.pool_tick, 1)
                    nc.gpsimd.indirect_dma_start(out=y_d, out_offset=bass.IndirectOffsetOnAxis(ap=who_out[b][:], axis=0),
                                                 in_=y[b][:], in_offset=None, bounds_check=NODES - 1,
                                                 oob_is_err=False).then_inc(y_stored[b], 16)

                gather(0, 0)
                gather(1, 1)
                split(0, 0, 1, False)
                split(0, 0, 2, True)
                split(1, 1, 1, False)
                gather(2, 0)

                def step(t, b, left):
                    if left >= 3:
                        gather(t + 3, 1 - b)
                    if left >= 2:
                        split(t + 2, b, 1, False)
                    if left >= 1:
                        split(t + 1, 1 - b, 2, True)
                    scatter(t, b)

                tiles_of(pool, SLOTS, step)
                for b in range(2):
                    pool.wait_ge(y_stored[b], 16 * ((SLOTS + 1 - b) // 2))

            @block.scalar
            def _(act):
                def split(t, b):
                    act.wait_ge(e.land_in[0], 16 * t + 16)
                    if not isinstance(t, int) or t >= 2:
                        act.wait_ge(e.up_sum, t + 1)
                    nc.scalar.copy(e.piece(b, "hi", 0), e.landed(0)).then_inc(e.split_hi[0], 1)

                def x_hi(t, b):
                    act.wait_ge(e.turned, t + 1)
                    act.wait_ge(e.up_sum, t + 1)
                    for h in range(2):
                        cp = nc.scalar.copy(e.xt[b]["hi"][:, 4 * h:4 * h + 4, :], e.ps_x[h][:])
                    cp.then_inc(e.xt_hi_set, 1)

                def gelu(t, b):
                    act.wait_ge(e.up_sum, t + 3)
                    act.wait_ge(e.gate_set, t + 1)
                    nc.scalar.activation(e.gelu[b][:], e.ps_ab[b][:, 0:INTER], ACT.Gelu).then_inc(e.gelu_set, 1)

                split(0, 0)
                x_hi(0, 0)
                split(1, 1)
                gelu(0, 0)
                x_hi(1, 1)

                def step(t, b, left):
                    act.wait_ge(e.g_turned, t + 1)
                    act.wait_ge(e.y_sum, t + 1)
                    nc.scalar.copy(e.gt["hi"][:], e.ps_g[:]).then_inc(e.gt_hi_set, 1)
                    if left >= 2:
                        split(t + 2, b)
                    if left >= 1:
                        gelu(t + 1, 1 - b)
                    if left >= 2:
                        x_hi(t + 2, b)
                    act.wait_ge(e.y_sum, t + 2)
                    if not isinstance(t, int) or t >= 2:
                        act.wait_ge(y_stored[b], 8 * t - 8 * b)
                    nc.scalar.copy(y[b][:], e.ps_y[:]).then_inc(y_set, 1)

                tiles_of(act, SLOTS, step)

            @block.vector
            def _(dve):
                dve.sem_inc(e.gate_set, 2)

                def x_lo(t, b):
                    dve.wait_ge(e.xt_hi_set, t + 1)
                    for h in range(2):
                        sub = nc.vector.tensor_tensor(e.xt[b]["lo"][:, 4 * h:4 * h + 4, :], e.ps_x[h][:],
                                                      e.xt[b]["hi"][:, 4 * h:4 * h + 4, :].bitcast(F32), ALU.subtract)
                    sub.then_inc(e.xt_lo_set, 1)

                def split(t, b):
                    for n in range(2):
                        dve.wait_ge(e.split_hi[n], t + 1)
                        nc.vector.tensor_tensor(e.piece(b, "lo", n), e.landed(n), e.piece(b, "hi", n).bitcast(F32),
                                                ALU.subtract).then_inc(e.split_lo[n], 1)

                def gate(t, b):
                    dve.wait_ge(e.gelu_set, t + 1)
                    if not isinstance(t, int) or t >= 2:
                        dve.wait_ge(e.g_turned, t - 1)
                    nc.vector.tensor_tensor(e.gate[b][:], e.gelu[b][:], e.ps_ab[b][:, INTER:2 * INTER],
                                            ALU.mult).then_inc(e.gate_set, 1)

                split(0, 0)
                x_lo(0, 0)
                split(1, 1)
                gate(0, 0)
                x_lo(1, 1)

                def step(t, b, left):
                    dve.wait_ge(e.gt_hi_set, t + 1)
                    nc.vector.tensor_tensor(e.gt["lo"][:], e.ps_g[:], e.gt["hi"][:].bitcast(F32),
                                            ALU.subtract).then_inc(e.gt_lo_set, 1)
                    if left >= 2:
                        split(t + 2, b)
                    if left >= 1:
                        gate(t + 1, 1 - b)
                    if left >= 2:
                        x_lo(t + 2, b)

                tiles_of(dve, SLOTS, step)

            @block.tensor
            def _(pe):
                pe.sem_inc(e.up_sum, 2)
                pe.sem_inc(e.y_sum, 1)

                def turn(t, b):
                    pe.wait_ge(x_in[b], 8 * t - 8 * b + 16)
                    if not isinstance(t, int) or t >= 1:
                        pe.wait_ge(e.xt_lo_set, t)
                    for k in range(KT):
                        mm = nc.tensor.transpose(e.ps_x[k // 4][:, k % 4, :], e.x[b][:, k * 128:(k + 1) * 128], ident[:])
                    mm.then_inc(e.turned, 1)

                def up(t, b):
                    pe.wait_ge(e.xt_lo_set, t + 1)
                    pe.wait_ge(e.gate_set, t + 1)
                    pe.wait_ge(e.split_lo[0], t + 1)
                    pe.wait_ge(e.split_lo[1], t + 1)
                    for k in range(KT):
                        for n, (l, r) in enumerate(SPLIT):
                            mm = nc.tensor.matmul(e.ps_ab[b][:], e.xt[b][l][:, k, :], e.w12[b][r][:, k, :],
                                                  start=(k == 0 and n == 0), stop=(k == KT - 1 and n == 2))
                    mm.then_inc(e.up_sum, 1)

                def down(t, b):
                    pe.wait_ge(e.gt_lo_set, t + 1)
                    pe.wait_ge(e.split_lo[2], t + 1)
                    if not isinstance(t, int) or t >= 1:
                        pe.wait_ge(y_set, t)
                    for half in range(2):
                        cols = slice(half * BANK, (half + 1) * BANK)
                        for k in range(2):
                            for n, (l, r) in enumerate(SPLIT):
                                mm = nc.tensor.matmul(e.ps_y[:, cols], e.gt[l][:, k, :], e.w3[b][r][:, k, cols],
                                                      start=(k == 0 and n == 0), stop=(k == 1 and n == 2))
                    mm.then_inc(e.y_sum, 1)

                turn(0, 0)
                up(0, 0)
                turn(1, 1)

                def step(t, b, left):
                    pe.wait_ge(e.gate_set, t + 3)
                    if not isinstance(t, int) or t >= 1:
                        pe.wait_ge(e.gt_lo_set, t)
                    for k in range(2):
                        mm = nc.tensor.transpose(e.ps_g[:, k, :], e.gate[b][:, k * 128:(k + 1) * 128], ident[:])
                    mm.then_inc(e.g_turned, 1)
                    if left >= 1:
                        up(t + 1, 1 - b)
                    if left >= 2:
                        turn(t + 2, b)
                    down(t, b)

                tiles_of(pe, SLOTS, step)


def finish(nc, X, y_d, out):
    with ExitStack() as ctx:
        c = Core(nc, ctx, "finish")
        y = c.sb("y", [P, TILES, DIM], F32)
        y_in = [c.sem(f"y_in{t}") for t in range(TILES)]
        added, stored = c.sem("added"), c.sem("out_stored")
        with nc.Block() as block:

            @block.sync
            def _(sp):
                for t in range(TILES):
                    sp.dma_start(y[:, t, :], y_d[t * P:(t + 1) * P, :]).then_inc(y_in[t], 16)
                for t in range(TILES):
                    sp.wait_ge(added, t + 1)
                    sp.dma_start(out[t * P:(t + 1) * P, :], y[:, t, :]).then_inc(stored, 16)
                sp.wait_ge(stored, 16 * TILES)

            @block.vector
            def _(dve):
                for t in range(TILES):
                    dve.wait_ge(y_in[t], 16)
                    nc.vector.tensor_tensor(y[:, t, :], y[:, t, :], X[:, t, :], ALU.add).then_inc(added, 1)


def program(nc, out, x, src, dst, W0, a_l, a_r, maker, up, cproj, W1g, b1g, w1s, w2s, w3s, W1, W2, W3, Wg):
    Core.spent.clear()

    def scratch(name, shape, dt=F32):
        return nc.dram_tensor(name, shape, dt, kind="Internal").ap()

    counts, counts_t = scratch("counts", (NODES, NODES), U16), scratch("counts_t", (NODES, NODES), U16)
    z_hi, z_lo = scratch("z_hi_d", (NODES, DIM)), scratch("z_lo_d", (NODES, DIM))
    xn_d, y_d = scratch("xn_d", (NODES, DIM)), scratch("y_d", (NODES, DIM))
    tokens_d = scratch("tokens_d", (SLOTS * SLOT, 1), I32)
    with ExitStack() as ctx:
        keep = Core(nc, ctx, "keep")
        X = keep.sb("X", [P, TILES, DIM], F32)
        ident = keep.sb("ident", [128, 128], F32)
        mean_var, rstd = keep.sb("mean_var", [P, TILES, 2], F32), keep.sb("rstd", [P, TILES], F32)
        el, er = keep.sb("el", [P, TILES, HEADS], F32), keep.sb("er", [P, TILES, HEADS], F32)
        dis = keep.sb("dis", [P, TILES], F32)
        logits = keep.sb("logits", [P, TILES, EXPERTS], F32)
        tokens, slot_expert = keep.sb("tokens", [SLOT, SLOTS], I32), keep.sb("slot_expert", [1, SLOTS], I32)
        constants(nc, keep, x, X, ident)
        count_edges(nc, src, dst, ident, counts, counts_t)
        layer_stats(nc, "stats0", X, mean_var, rstd)
        node_linear(nc, "attention", X, mean_var, rstd, ident, W0, z_hi, z_lo, (a_l, a_r, el, er))
        attention(nc, X, ident, counts, counts_t, z_hi, z_lo, el, er, dis)
        layer_stats(nc, "stats1", X, mean_var, rstd)
        rails(nc, X, mean_var, rstd, ident, maker, up, cproj)
        layer_stats(nc, "stats2", X, mean_var, rstd)
        node_linear(nc, "graph", X, mean_var, rstd, ident, W1g, z_hi, z_lo, (b1g, dis))
        aggregate(nc, X, ident, counts, z_hi, z_lo, dis)
        recycle(nc)
        layer_stats(nc, "stats3", X, mean_var, rstd)
        shared_expert(nc, X, mean_var, rstd, ident, w1s, w2s, w3s, Wg, xn_d, logits)
        route(nc, logits, ident, tokens_d, tokens, slot_expert)
        routed_experts(nc, ident, W1, W2, W3, xn_d, y_d, tokens, slot_expert)
        finish(nc, X, y_d, out)


def kernel(x, src, dst, L0_gnn_W, L0_gnn_a_l, L0_gnn_a_r, L0_ffn_rail_maker, L0_ffn_rail_up_proj, L0_ffn_w_cproj,
           L1_gnn_W, L1_gnn_b, L1_ffn_w1s, L1_ffn_w2s, L1_ffn_w3s, L1_ffn_W1, L1_ffn_W2, L1_ffn_W3, L1_ffn_Wg):
    import numpy as np
    import concourse.bacc as bacc
    from concourse.bass_utils import run_bass_kernel_spmd

    laid = {
        "x": np.asarray(x),
        "src": np.asarray(src).reshape(CHUNKS, P).T,
        "dst": np.asarray(dst).reshape(CHUNKS, P).T,
        "W0": np.asarray(L0_gnn_W).transpose(1, 0, 2).reshape(DIM, DIM),
        "a_l": np.asarray(L0_gnn_a_l).reshape(DIM),
        "a_r": np.asarray(L0_gnn_a_r).reshape(DIM),
        "maker": np.asarray(L0_ffn_rail_maker).transpose(1, 3, 0, 2),
        "up": np.asarray(L0_ffn_rail_up_proj).transpose(1, 3, 0, 2),
        "cproj": np.asarray(L0_ffn_w_cproj).T,
        "W1g": np.asarray(L1_gnn_W).T,
        "b1g": np.asarray(L1_gnn_b),
        "w1s": np.asarray(L1_ffn_w1s), "w2s": np.asarray(L1_ffn_w2s), "w3s": np.asarray(L1_ffn_w3s),
        "W1": np.asarray(L1_ffn_W1), "W2": np.asarray(L1_ffn_W2), "W3": np.asarray(L1_ffn_W3),
        "Wg": np.asarray(L1_ffn_Wg),
    }
    laid = {name: np.ascontiguousarray(a) for name, a in laid.items()}
    nc = bacc.Bacc("TRN2", target_bir_lowering=False, num_devices=1)
    args = {name: nc.dram_tensor(name, a.shape, mybir.dt.from_np(a.dtype), kind="ExternalInput").ap()
            for name, a in laid.items()}
    out = nc.dram_tensor("out", (NODES, DIM), F32, kind="ExternalOutput").ap()
    program(nc, out, **args)
    result = run_bass_kernel_spmd(nc, [laid], core_ids=[0])
    return result.results[0]["out"]
```
